# Optimizing a Trainium2 kernel written in Bass

```python
import numpy as np
import jax
import jax.numpy as jnp

def _softmax(x, axis=-1):
    return jax.nn.softmax(x, axis=axis)

def _gelu(x):
    return jax.nn.gelu(x, approximate=True)

def _silu(x):
    return jax.nn.silu(x)

def _sigmoid(x):
    return jax.nn.sigmoid(x)

def _layernorm(x, axis=-1, eps=1e-05):
    m = jnp.mean(x, axis=axis, keepdims=True)
    v = jnp.var(x, axis=axis, keepdims=True)
    return (x - m) / jnp.sqrt(v + eps)

def _scatter_add(tgt, idx, src, axis=0):
    return tgt.at[idx].add(src)

def _segment_sum(src, seg, n):
    return jax.ops.segment_sum(src, seg, n)
kernel_name = 'mk_gnn_resnorm_d2_gnn_r8_98c6ae'

def setup_inputs(seed: int=0):
    np.random.seed(seed)
    _w = jnp.asarray

    def _rec_inputs():
        import jax
        import jax.numpy as jnp
        _gk = jax.random.key(seed)
        x = -0.0003713 + 1 * jax.random.normal(jax.random.fold_in(_gk, 1), (6250, 128), jnp.float32)
        _s = jax.random.randint(jax.random.fold_in(_gk, 2), (100000,), 0, 6250, jnp.int32)
        _d = jax.random.randint(jax.random.fold_in(_gk, 3), (100000,), 0, 6250, jnp.int32)
        _loop = jnp.arange(6250, dtype=jnp.int32)
        src = jnp.concatenate([_s, _d, _loop])
        dst = jnp.concatenate([_d, _s, _loop])
        _o = jnp.argsort(dst, stable=True)
        src = src[_o]
        dst = dst[_o]
        edge_type_64 = jax.random.randint(jax.random.fold_in(_gk, 12), (206250,), 0, 64, jnp.int32)
        edge_weight = jax.random.uniform(jax.random.fold_in(_gk, 13), (206250,), jnp.float32, 0.0, 0.999998)
        return (x, src, dst, edge_type_64, edge_weight)
    x, src, dst, edge_type_64, edge_weight = _rec_inputs()

    def _L0_gnn_setup():
        import jax, jax.numpy as jnp
        import numpy as np
        EPS = 0.0
        key = jax.random.key(seed)
        kx, ke, kw, k1, k2 = jax.random.split(key, 5)
        N, E, D, H = (12500, 75000, 128, 128)
        x = jax.random.normal(kx, (N, D), dtype=jnp.float32)
        edge_index = jax.random.randint(ke, (2, E), 0, N, dtype=jnp.int64)
        edge_weight = jax.random.uniform(kw, (E,), dtype=jnp.float32)
        W1 = jax.random.normal(k1, (D, H), dtype=jnp.float32) * (1.0 / np.sqrt(D))
        b1 = jnp.zeros((H,), dtype=jnp.float32)
        W2 = jax.random.normal(k2, (H, D), dtype=jnp.float32) * (1.0 / np.sqrt(H))
        b2 = jnp.zeros((D,), dtype=jnp.float32)
        return {'x': x, 'edge_index': edge_index, 'edge_weight': edge_weight, 'W1': W1, 'b1': b1, 'W2': W2, 'b2': b2}
    _L0_gnn_all = _L0_gnn_setup()
    _L0_gnn_in = {k: v for k, v in _L0_gnn_all.items() if k in ('W1', 'b1', 'W2', 'b2')}
    del _L0_gnn_all

    def _L1_gnn_setup():
        import jax, jax.numpy as jnp
        import numpy as np
        N_HOPS = 3
        N_ENTITIES = 12500
        EMB = 128
        N_EDGES = 75000
        N_REL = 64
        key = jax.random.key(seed)
        k1, k2, k3, k4, k5, k6 = jax.random.split(key, 6)
        entity_emb = jax.random.normal(k1, (N_ENTITIES, EMB), dtype=jnp.float32)
        edge_emb = jax.random.normal(k2, (N_REL, EMB), dtype=jnp.float32)
        q_w = jax.random.normal(k3, (EMB, EMB), dtype=jnp.float32) * (1.0 / np.sqrt(EMB))
        k_w = jax.random.normal(k4, (EMB, EMB), dtype=jnp.float32) * (1.0 / np.sqrt(EMB))
        edge_index = jax.random.randint(k5, (2, N_EDGES), 0, N_ENTITIES, dtype=jnp.int64)
        edge_type = jax.random.randint(k6, (N_EDGES,), 0, N_REL, dtype=jnp.int64)
        return {'entity_emb': entity_emb, 'edge_emb': edge_emb, 'q_w': q_w, 'k_w': k_w, 'edge_index': edge_index, 'edge_type': edge_type, 'mess_dropout': 0}
    _L1_gnn_all = _L1_gnn_setup()
    _L1_gnn_in = {k: v for k, v in _L1_gnn_all.items() if k in ('edge_emb', 'q_w', 'k_w')}
    del _L1_gnn_all
    return {'x': x, 'src': src, 'dst': dst, 'edge_type_64': edge_type_64, 'edge_weight': edge_weight, 'L0_gnn_W1': _L0_gnn_in['W1'], 'L0_gnn_b1': _L0_gnn_in['b1'], 'L0_gnn_W2': _L0_gnn_in['W2'], 'L0_gnn_b2': _L0_gnn_in['b2'], 'L1_gnn_edge_emb': _L1_gnn_in['edge_emb'], 'L1_gnn_q_w': _L1_gnn_in['q_w'], 'L1_gnn_k_w': _L1_gnn_in['k_w']}

def reference(x, src, dst, edge_type_64, edge_weight, L0_gnn_W1, L0_gnn_b1, L0_gnn_W2, L0_gnn_b2, L1_gnn_edge_emb, L1_gnn_q_w, L1_gnn_k_w):
    import jax
    import jax.numpy as jnp

    def _L0_gnn_ref(x, edge_index, edge_weight, W1, b1, W2, b2):
        import jax, jax.numpy as jnp
        import numpy as np
        EPS = 0.0
        N = x.shape[0]
        src, dst = (edge_index[0], edge_index[1])
        msg = edge_weight[:, None] * x[src]
        agg = jax.ops.segment_sum(msg, dst, num_segments=N)
        out = (1.0 + EPS) * x + agg
        h = jax.nn.relu(out @ W1 + b1)
        return h @ W2 + b2

    def _L1_gnn_ref(entity_emb, edge_emb, q_w, k_w, edge_index, edge_type, mess_dropout):
        import jax, jax.numpy as jnp
        import numpy as np
        N_HOPS = 3
        N_ENTITIES = 12500
        EMB = 128
        N_EDGES = 75000
        N_REL = 64
        head = edge_index[0]
        tail = edge_index[1]
        rel = edge_emb[edge_type]
        n = entity_emb.shape[0]
        agg = entity_emb
        out = jnp.zeros_like(entity_emb)
        for _ in range(N_HOPS):
            h = agg[head]
            t = agg[tail]
            left = h @ q_w
            right = jnp.tanh(rel * t @ k_w)
            att = jnp.sum(left * right, axis=1)
            seg_max = jax.ops.segment_max(att, head, num_segments=n)
            e = jnp.exp(att - seg_max[head])
            seg_sum = jax.ops.segment_sum(e, head, num_segments=n)
            w = e / seg_sum[head]
            msg = w[:, None] * rel * t
            summed = jax.ops.segment_sum(msg, head, num_segments=n)
            cnt = jax.ops.segment_sum(jnp.ones_like(att), head, num_segments=n)
            agg = summed / jnp.maximum(cnt, 1.0)[:, None]
            norm = jnp.linalg.norm(agg, axis=1, keepdims=True)
            agg = agg / jnp.maximum(norm, 1e-12)
            out = out + agg + entity_emb
        return out
    edge_index = jnp.stack([src, dst])
    x = _layernorm(x + _L0_gnn_ref(x, edge_index, edge_weight, L0_gnn_W1, L0_gnn_b1, L0_gnn_W2, L0_gnn_b2), axis=-1)
    x = _layernorm(x + _L1_gnn_ref(x, L1_gnn_edge_emb, L1_gnn_q_w, L1_gnn_k_w, edge_index, edge_type_64, 0), axis=-1)
    return x

_drawn_inputs = setup_inputs


def setup_inputs(seed=0):
    import zlib

    import numpy as np

    out = dict(_drawn_inputs(seed))
    spreads = {'L0_gnn_b1': (0.0, 0.304), 'L0_gnn_b2': (0.0, 0.1)}
    factors = {}
    for name, (base, spread) in spreads.items():
        noise = np.random.default_rng([zlib.crc32(name.encode()), seed]).standard_normal(out[name].shape)
        drawn = base * np.exp(spread * noise) if base else spread * noise
        out[name] = jnp.asarray(drawn.astype(out[name].dtype))
    for name, factor in factors.items():
        out[name] = (out[name] * factor).astype(out[name].dtype)
    return out
```

```python
from contextlib import ExitStack, nullcontext
from math import ceil

import concourse.bass as bass
from concourse import mybir

ALU = mybir.AluOpType
ACT = mybir.ActivationFunctionType
AX_X = mybir.AxisListType.X
F32 = mybir.dt.float32
BF16 = mybir.dt.bfloat16
I32 = mybir.dt.int32

P = 128
BANK = 512
GROUP = BANK // P
UNROLL = 4
HOPS = 3
LN_EPS = 1e-5
BIG = 1e30
START = 3e38
SKIP = 1.0e6


class Sizes:

    def __init__(self, nodes, edges, dim, types):
        self.N, self.E, self.D, self.T = nodes, edges, dim, types
        self.tiles = ceil(ceil(edges / P) / (GROUP * UNROLL)) * GROUP * UNROLL
        self.groups = self.tiles // GROUP
        self.tblocks = ceil(self.tiles / P)
        self.ntiles = ceil((nodes + 1) / P)
        self.NP = self.ntiles * P
        self.rblocks = ceil((nodes + 1 + self.tiles) / P)
        self.R = self.rblocks * P
        self.RW = self.R + P


class Sem:

    def __init__(self, handle):
        self.handle, self.base = handle, 0


class Chain:

    def __init__(self, nc, count, pool_count, only=None):
        self.nc, self.count, self.pool_count, self.stages = nc, count, pool_count, [[]]
        self.only = only or (lambda engine, name: nullcontext())

    def then(self):
        self.stages.append([])

    def do(self, engine, make, dma=False):
        self.stages[-1].append((engine, make, dma))

    def run(self):
        before, at, pool_at = [], self.count.base, self.pool_count.base
        for stage in self.stages:
            before.append((at, pool_at))
            for engine, _, dma in stage:
                if dma and engine == "gpsimd":
                    pool_at += 16
                else:
                    at += 16 if dma else 1
        before.append((at, pool_at))

        def play(name):
            def program(e):
                with self.only(e, name):
                    stages(e)

            def stages(e):
                seen, pool_seen = self.count.base, self.pool_count.base
                last = [[]] if name == "sync" else []
                for k, stage in enumerate(self.stages + last):
                    own = [s for s in stage if s[0] == name]
                    if not own and not (last and k == len(self.stages)):
                        continue
                    if before[k][0] > seen:
                        seen = before[k][0]
                        e.wait_ge(self.count.handle, seen)
                    if before[k][1] > pool_seen:
                        pool_seen = before[k][1]
                        e.wait_ge(self.pool_count.handle, pool_seen)
                    for _, make, dma in own:
                        s = self.pool_count if dma and name == "gpsimd" else self.count
                        make(e).then_inc(s.handle, 16 if dma else 1)

            return program

        with self.nc.Block() as block:
            for name in ("sync", "scalar", "vector", "tensor", "gpsimd"):
                getter = {"sync": block.sync, "scalar": block.scalar, "vector": block.vector,
                          "tensor": block.tensor, "gpsimd": block.gpsimd}[name]
                getter(play(name))
        self.count.base, self.pool_count.base = at, pool_at


class Step:

    def __init__(self, e, i, groups, turn=None, rates=None, spare=None):
        self.e, self.i, self.groups, self.turn = e, i, groups, turn
        self.rates, self.spare, self.used = rates, spare, 0

    def live(self, lag):
        return self.turn is not None or 0 <= self.i - lag < self.groups

    def slot(self, lag, ring):
        return (self.i - lag) % ring

    def at(self, f):
        if self.turn is None:
            return f(self.i)
        rate = f(self.i + UNROLL) - f(self.i)
        return self.turn * rate + f(self.i)

    def wait(self, *conditions, apart=False):
        found = []
        for s, f in conditions:
            if f(self.i) <= 0:
                assert self.turn is None
                continue
            if self.turn is None:
                found.append((s, s.base + f(self.i)))
                continue
            rate = f(self.i + UNROLL) - f(self.i)
            r = self.spare[self.used % len(self.spare)]
            self.used += 1
            self.e.reg_add(r, self.rates[rate], s.base + f(self.i) - rate)
            found.append((s, r))
        if apart and self.turn is not None:
            s, f = conditions[-1]
            self.e.wait_ge(s.handle, s.base + f(self.i))
        for s, value in found:
            self.e.wait_ge(s.handle, value)


def ring_count(lag, ring, inc):
    return lambda i: inc * ((i - lag) // ring + 1) if i >= lag else 0


def done(lag, per=1):
    return lambda i: per * (i - lag + 1) if i >= lag else 0


def pipeline(e, name, step, groups, depth, rates):
    first = ceil(depth / UNROLL) * UNROLL
    turns = (groups - first) // UNROLL
    for i in range(first):
        step(Step(e, i, groups))
    regs = {}
    for rate in rates:
        regs[rate] = e.alloc_register(f"{name}_rate{rate}")
        e.reg_mov(regs[rate], rate)
    spare = [e.alloc_register(f"{name}_until{n}") for n in range(8)]
    with e.Fori(0, turns) as turn:
        for b in range(UNROLL):
            step(Step(e, first + b, groups, turn, regs, spare))
        for rate in rates:
            e.reg_add(regs[rate], regs[rate], rate)
    for r in [*regs.values(), *spare]:
        e.free_register(r)
    for i in range(first + turns * UNROLL, groups + depth):
        step(Step(e, i, groups))


def gnn_two_layers(nc, x, src, dst, edge_type, edge_weight, w1, b1, w2, b2, edge_emb, q_w, k_w, out,
                   debug=None):
    z = Sizes(x.shape[0], src.shape[0], x.shape[1], edge_emb.shape[0])
    assert z.D == P and z.T * 2 == P and z.groups % UNROLL == 0
    top = ExitStack()
    with top:
        def sem(name):
            return Sem(top.enter_context(nc.semaphore(name)))

        def tensor(ctx, name, shape, dt=F32):
            return ctx.enter_context(nc.sbuf_tensor(name, shape, dt))

        def dram(name, shape, dt=F32):
            return nc.dram_tensor(name, shape, dt, kind="Internal").ap()

        bank = [top.enter_context(nc.psum_tensor(f"bank{i}", [P, BANK], F32)) for i in range(8)]
        count, pool_count = sem("chain"), sem("chain_pool")

        def chain():
            return Chain(nc, count, pool_count)

        key_rows = dram("key_rows", (z.tblocks * P, 2, P))
        tile_rows = dram("tile_rows", (z.tblocks * P, 2, P), BF16)
        first_run = dram("first_run", (z.tblocks * P,), I32)
        node_words = dram("node_words", (3, P // 2, P))
        run_keys = dram("run_keys", (z.RW, 1))
        run_node = dram("run_node", (z.R,), I32)
        run_goes_on = dram("run_goes_on", (z.R,), BF16)
        run_out = dram("run_out", (z.R, z.D))
        run_stats = dram("run_stats", (2, z.RW))
        node_rows = dram("node_rows", (z.NP, z.D))
        entity_rows = dram("entity_rows", (z.NP, z.D))
        by_dst = dram("by_dst", (P * z.tiles, 4))
        by_src = dram("by_src", (P * z.tiles, 4))

        ident = tensor(top, "ident", [P, P])
        below = tensor(top, "below", [P, P])
        above = tensor(top, "above", [P, P])
        ones = tensor(top, "ones", [P, P])
        column = tensor(top, "column", [P, P])
        row = tensor(top, "row", [P, 1])
        row_half = tensor(top, "row_half", [P, 1])
        c = chain()
        c.do("gpsimd", lambda e: e.memset(ones[:, :], 1.0))
        c.do("gpsimd", lambda e: e.iota(column[:, :], [[1, P]], base=0, channel_multiplier=0,
                                        allow_small_or_imprecise_dtypes=True))
        c.do("gpsimd", lambda e: e.iota(row[:, :], [[1, 1]], base=0, channel_multiplier=1,
                                        allow_small_or_imprecise_dtypes=True))
        c.then()
        c.do("vector", lambda e: e.tensor_scalar(ident[:, :], column[:, :], row[:, 0:1], None, ALU.is_equal))
        c.do("vector", lambda e: e.tensor_scalar(below[:, :], column[:, :], row[:, 0:1], None, ALU.is_lt))
        c.do("vector", lambda e: e.tensor_scalar(above[:, :], column[:, :], row[:, 0:1], None, ALU.is_gt))
        c.do("vector", lambda e: e.tensor_scalar(row_half[:, :], row[:, :], float(z.T), float(-z.T), ALU.is_ge, ALU.mult))
        c.then()
        c.do("vector", lambda e: e.tensor_tensor(row_half[:, :], row_half[:, :], row[:, :], ALU.add))
        c.run()

        def load_edges(c, to, array, skip=0):
            n = z.E - skip
            whole_rows = n // z.tiles
            c.do("sync", lambda e: e.dma_start(to[0:whole_rows, :], array[skip:skip + whole_rows * z.tiles].rearrange("(p k) -> p k", k=z.tiles)), dma=True)
            if n > whole_rows * z.tiles:
                c.do("sync", lambda e: e.dma_start(to[whole_rows:whole_rows + 1, 0:n - whole_rows * z.tiles],
                                                   array[skip + whole_rows * z.tiles:z.E].unsqueeze(0)), dma=True)

        def rows_of(c, columns, blocks, to):
            c.then()
            for b in range(blocks):
                c.do("tensor", lambda e, b=b: e.transpose(bank[b // GROUP][:, b % GROUP * P:b % GROUP * P + P],
                                                          columns[:, b * P:b * P + P], ident[:, :]))
            c.then()
            for b in range(0, blocks, GROUP):
                n = min(GROUP, blocks - b)
                engine = "vector" if b % (2 * GROUP) else "scalar"
                c.do(engine, copy(to[:, b:b + n, :], bank[b // GROUP][:, 0:n * P].rearrange("p (b q) -> p b q", b=n), engine))

        def copy(to, of, engine, scale=None):
            if engine == "scalar":
                return lambda e: e.activation(to, of, ACT.Copy, scale=1.0 if scale is None else scale)
            if scale is not None:
                return lambda e: e.tensor_scalar(to, of, scale, None, ALU.mult)
            return lambda e: e.tensor_copy(to, of)

        s_hot, s_hist = sem("s_hot"), sem("s_hist")
        s_copy_idx, s_weights, s_mm, s_write = sem("s_copy_idx"), sem("s_weights"), sem("s_mm"), sem("s_write")
        sp_gather = [sem(f"sp_gather{i}") for i in range(UNROLL)]
        sorted_count, sorted_pool_count = sem("sorted_chain"), sem("sorted_chain_pool")

        def sort_edges(name, key_of, other_of, third_of, third_dt, to, often_sorted=False):
            H = P // 2
            s_place_hot, s_look, s_rank, s_math = (sem(f"{name}_s_{n}") for n in ("place_hot", "look", "rank", "math"))
            s_table, s_step, s_load = (sem(f"{name}_s_{n}") for n in ("table", "step", "load"))
            s_rows = [sem(f"{name}_s_rows{i}") for i in range(UNROLL)]
            sp_scatter = [sem(f"{name}_sp_scatter{i}") for i in range(UNROLL)]
            with ExitStack() as ctx:
                unsorted = tensor(ctx, f"{name}_unsorted", [1, 1], I32)
                turn_to = {"sync": mybir.EngineType.SP, "scalar": mybir.EngineType.Activation, "vector": mybir.EngineType.DVE,
                           "tensor": mybir.EngineType.PE, "gpsimd": mybir.EngineType.Pool}

                def if_unsorted(e, engine, wanted=1):
                    if not often_sorted:
                        return nullcontext()
                    _, flag = nc.values_load_multi_w_load_instructions(unsorted[0:1, 0:1], engines=[turn_to[engine]], min_val=0, max_val=1,
                                                                       skip_runtime_bounds_check_because="a comparison's result")
                    return e.If(flag[0] == wanted)

                words = tensor(ctx, f"{name}_words", [P, z.tiles, 4])
                raw = tensor(ctx, f"{name}_raw", [P, z.tiles], I32)
                raw_other = tensor(ctx, f"{name}_raw_other", [P, z.tiles], I32)
                raw_third = tensor(ctx, f"{name}_raw_third", [P, z.tiles], third_dt)
                low = tensor(ctx, f"{name}_low", [P, z.tblocks * P])
                high = tensor(ctx, f"{name}_high", [P, z.tblocks * P])
                key = tensor(ctx, f"{name}_key", [P, z.tblocks * P])
                turned = tensor(ctx, f"{name}_turned", [P, z.tblocks, P])
                hot_low = tensor(ctx, f"{name}_hot_low", [P, 2, GROUP, P], BF16)
                hot_high = tensor(ctx, f"{name}_hot_high", [P, 2, GROUP, H], BF16)
                counts = tensor(ctx, f"{name}_counts", [H, P])
                offsets = tensor(ctx, f"{name}_offsets", [H, P])

                c = chain()
                c.do("gpsimd", lambda e: e.memset(raw[:, :], z.N))
                c.do("gpsimd", lambda e: e.memset(raw_other[:, :], 0))
                c.do("vector", lambda e: e.memset(raw_third[:, :], 0))
                c.do("vector", lambda e: e.memset(words[:, :, 3], 0))
                c.do("vector", lambda e: e.memset(key[:, :], float(z.N)))
                c.then()
                load_edges(c, raw, key_of)
                load_edges(c, raw_other, other_of)
                load_edges(c, raw_third, third_of)
                c.then()
                c.do("vector", lambda e: e.tensor_copy(key[:, 0:z.tiles], raw[:, :]))
                c.do("vector", lambda e: e.tensor_copy(words[:, :, 0], raw_other[:, :]))
                c.do("vector", lambda e: e.tensor_copy(words[:, :, 2], raw_third[:, :]))
                c.then()
                c.do("scalar", copy(words[:, :, 1], key[:, 0:z.tiles], "scalar"))
                c.do("vector", lambda e: e.tensor_scalar(raw_other[:, :], raw[:, :], 7, None, ALU.arith_shift_right))
                c.do("vector", lambda e: e.tensor_scalar(raw[:, :], raw[:, :], P - 1, None, ALU.bitwise_and))
                c.then()
                c.do("vector", lambda e: e.memset(high[:, :], 0.0))
                c.do("vector", lambda e: e.tensor_copy(low[:, 0:z.tiles], raw[:, :]))
                c.then()
                c.do("vector", lambda e: e.tensor_copy(high[:, 0:z.tiles], raw_other[:, :]))
                for w, columns in ((0, key), (1, high)):
                    rows_of(c, columns, z.tblocks, turned)
                    c.then()
                    c.do("sync", lambda e, w=w: e.dma_start(key_rows.rearrange("(b t) w p -> w t b p", t=P)[w], turned[:, :, :]), dma=True)
                if often_sorted:
                    following = tensor(ctx, f"{name}_following", [P, z.tiles])
                    falls = tensor(ctx, f"{name}_falls", [P, 1])
                    c.do("gpsimd", lambda e: e.memset(raw[:, :], z.N))
                    c.then()
                    load_edges(c, raw, key_of, skip=1)
                    c.then()
                    c.do("vector", lambda e: e.tensor_copy(following[:, :], raw[:, :]))
                    c.then()
                    c.do("vector", lambda e: e.tensor_tensor(following[:, :], key[:, 0:z.tiles], following[:, :], ALU.is_gt))
                    c.then()
                    c.do("vector", lambda e: e.tensor_reduce(falls[:, :], following[:, :], AX_X, ALU.max))
                    c.then()
                    c.do("tensor", lambda e: e.matmul(bank[7][0:1, 0:1], falls[:, :], ones[:, 0:1], start=True, stop=True))
                    c.then()
                    c.do("vector", lambda e: e.tensor_scalar(unsorted[:, :], bank[7][0:1, 0:1], 1.0, None, ALU.is_ge))
                c.run()

                def hot(e, slot, cols):
                    e.tensor_tensor(hot_low[:, slot, :, :], column[:, :].unsqueeze(1).to_broadcast([P, GROUP, P]),
                                    low[:, cols].unsqueeze(2).to_broadcast([P, GROUP, P]), ALU.is_equal)
                    return e.tensor_tensor(hot_high[:, slot, :, :], column[:, 0:H].unsqueeze(1).to_broadcast([P, GROUP, H]),
                                           high[:, cols].unsqueeze(2).to_broadcast([P, GROUP, H]), ALU.is_equal)

                def vector_hist(s):
                    if s.live(0):
                        cols = bass.ds(s.at(lambda i: GROUP * i), GROUP)
                        s.wait((s_hist, done(2)))
                        hot(s.e, s.slot(0, 2), cols).then_inc(s_hot.handle, 1)

                def tensor_hist(s):
                    if s.live(0):
                        s.wait((s_hot, done(0)))
                        for t in range(GROUP):
                            mm = s.e.matmul(bank[0][0:H, 0:P], hot_high[:, s.slot(0, 2), t, :], hot_low[:, s.slot(0, 2), t, :],
                                            start=(s.turn is None and s.i == 0 and t == 0), stop=True, skip_group_check=True)
                        mm.then_inc(s_hist.handle, 1)

                with nc.Block() as block:
                    @block.vector
                    def _(e):
                        pipeline(e, f"{name}_hv", vector_hist, z.groups, 2, (UNROLL,))

                    @block.tensor
                    def _(e):
                        pipeline(e, f"{name}_ht", tensor_hist, z.groups, 2, (UNROLL,))
                for s in (s_hot, s_hist):
                    s.base += z.groups

                a = tensor(ctx, f"{name}_a", [H, P])
                b = tensor(ctx, f"{name}_b", [H, P])
                nruns = tensor(ctx, f"{name}_nruns", [H, P])
                some = tensor(ctx, f"{name}_some", [H, P])
                ai = tensor(ctx, f"{name}_ai", [H, P], I32)
                bi = tensor(ctx, f"{name}_bi", [H, P], I32)

                def prefix(c, of, to):
                    c.then()
                    c.do("vector", lambda e: e.tensor_tensor_scan(to, ones[0:H, :], of, 0.0, ALU.mult, ALU.add))
                    c.then()
                    c.do("tensor", lambda e: e.matmul(bank[1][0:H, 0:1], above[0:H, 0:H], to[:, P - 1:P], start=True, stop=True))
                    c.then()
                    c.do("vector", lambda e: e.tensor_tensor(to, to, of, ALU.subtract))
                    c.then()
                    c.do("vector", lambda e: e.tensor_scalar(to, to, bank[1][0:H, 0:1], None, ALU.add))

                c = chain()
                c.do("vector", lambda e: e.tensor_copy(counts[:, :], bank[0][0:H, 0:P]))
                prefix(c, counts[:, :], offsets[:, :])
                c.then()
                c.do("vector", lambda e: e.tensor_copy(ai[:, :], offsets[:, :]))
                c.do("vector", lambda e: e.tensor_tensor(a[:, :], offsets[:, :], counts[:, :], ALU.add))
                c.do("vector", lambda e: e.tensor_scalar(some[:, :], counts[:, :], 1.0, None, ALU.is_ge))
                c.then()
                c.do("vector", lambda e: e.tensor_scalar(bi[:, :], a[:, :], -1.0, None, ALU.add))
                c.do("vector", lambda e: e.tensor_scalar(ai[:, :], ai[:, :], 7, None, ALU.arith_shift_right))
                c.then()
                c.do("vector", lambda e: e.tensor_scalar(bi[:, :], bi[:, :], 7, None, ALU.arith_shift_right))
                c.do("vector", lambda e: e.tensor_copy(a[:, :], ai[:, :]))
                c.then()
                c.do("vector", lambda e: e.tensor_copy(b[:, :], bi[:, :]))
                c.then()
                c.do("vector", lambda e: e.tensor_tensor(b[:, :], b[:, :], a[:, :], ALU.subtract))
                c.then()
                c.do("vector", lambda e: e.scalar_tensor_tensor(nruns[:, :], b[:, :], 1.0, some[:, :], ALU.add, ALU.mult))
                prefix(c, nruns[:, :], a[:, :])
                c.then()
                c.do("vector", lambda e: e.tensor_scalar(some[:, :], some[:, :], -SKIP, SKIP, ALU.mult, ALU.add))
                c.then()
                c.do("vector", lambda e: e.tensor_tensor(a[:, :], a[:, :], some[:, :], ALU.add))
                c.then()
                c.do("vector", lambda e: e.scalar_tensor_tensor(b[:, :], a[:, :], -1.0, nruns[:, :], ALU.add, ALU.add))
                c.then()
                c.do("sync", lambda e: e.dma_start(node_words[0], counts[:, :]), dma=True)
                c.do("sync", lambda e: e.dma_start(node_words[1], a[:, :]), dma=True)
                c.do("sync", lambda e: e.dma_start(node_words[2], b[:, :]), dma=True)
                c.do("tensor", lambda e: e.matmul(bank[0][0:H, 0:P], ident[0:H, 0:H], offsets[:, :], start=True, stop=True))
                c.run()

                rows_in = tensor(ctx, f"{name}_rows_in", [P, UNROLL, GROUP, 2, P])
                same = tensor(ctx, f"{name}_same", [P, 2, GROUP, P])
                hot_rows = tensor(ctx, f"{name}_hot_rows", [H, 2, GROUP, P])
                table = tensor(ctx, f"{name}_table", [H, 2, GROUP, P])
                waste = tensor(ctx, f"{name}_waste", [P, 2, GROUP, P])
                rank = tensor(ctx, f"{name}_rank", [P, 2, GROUP])
                base = tensor(ctx, f"{name}_base", [P, 2, GROUP])
                place = tensor(ctx, f"{name}_place", [P, 3, GROUP], I32)
                place_to = tensor(ctx, f"{name}_place_to", [P, UNROLL, GROUP], I32)
                load = tensor(ctx, f"{name}_load", [P, UNROLL, GROUP, 4])
                krows = key_rows.rearrange("t w p -> (t w p)")

                def sync_rows(s):
                    if s.live(0):
                        at = s.at(lambda i: GROUP * 2 * P * i)
                        s.wait((s_place_hot, done(UNROLL)))
                        s.e.dma_start(rows_in[:, s.slot(0, UNROLL), :, :, :].rearrange("q t w p -> q (t w p)"),
                                      krows[bass.ds(at, GROUP * 2 * P)].partition_broadcast(P)).then_inc(s_rows[s.slot(0, UNROLL)].handle, 16)

                def vector_place(s):
                    e = s.e
                    if s.live(2):
                        g2, g4 = s.slot(2, 2), s.slot(2, UNROLL)
                        s.wait((s_look, done(2)), (s_math, done(3, 4)), (sp_scatter[g4], ring_count(2 + UNROLL, UNROLL, 16 * GROUP)))
                        for t in range(GROUP):
                            e.tensor_tensor_reduce(waste[:, 0, t, :], same[:, g2, t, :], below[:, :], 1.0, 0.0, ALU.mult, ALU.add,
                                                   rank[:, g2, t:t + 1])
                            last = e.tensor_tensor_reduce(waste[:, 1, t, :], bank[2 + g2][:, t * P:t * P + P], hot_low_late[:, g4, t, :], 1.0, 0.0,
                                                          ALU.mult, ALU.add, base[:, g2, t:t + 1])
                        last.then_inc(s_rank.handle, 1)
                        s.wait((s_rank, done(2)))
                        e.tensor_tensor(place[:, 0, :], rank[:, g2, :], base[:, g2, :], ALU.add).then_inc(s_math.handle, 1)
                        s.wait((s_math, lambda i: 4 * (i - 2) + 1))
                        e.tensor_scalar(place[:, 1, :], place[:, 0, :], 7, None, ALU.arith_shift_right).then_inc(s_math.handle, 1)
                        e.tensor_scalar(place[:, 2, :], place[:, 0, :], P - 1, None, ALU.bitwise_and).then_inc(s_math.handle, 1)
                        s.wait((s_math, lambda i: 4 * (i - 2) + 3))
                        e.scalar_tensor_tensor(place_to[:, g4, :], place[:, 2, :], float(z.tiles), place[:, 1, :], ALU.mult, ALU.add)\
                            .then_inc(s_math.handle, 1)
                    if s.live(0):
                        g2, g4 = s.slot(0, 2), s.slot(0, UNROLL)
                        cols = bass.ds(s.at(lambda i: GROUP * i), GROUP)
                        s.wait((s_step, done(2, GROUP)), (s_look, done(2)), (s_rank, done(2)), (s_rows[g4], ring_count(0, UNROLL, 16)))
                        hot_high_only(e, g2, cols)
                        hot_low_kept(e, g4, cols)
                        e.tensor_scalar(hot_rows[:, g2, :, :], rows_in[0:H, g4, :, 1, :], row[0:H, 0:1], None, ALU.is_equal)
                        e.tensor_tensor(same[:, g2, :, :], rows_in[:, g4, :, 0, :],
                                        key[:, cols].unsqueeze(2).to_broadcast([P, GROUP, P]), ALU.is_equal).then_inc(s_place_hot.handle, 1)

                hot_low_late = tensor(ctx, f"{name}_hot_low_late", [P, UNROLL, GROUP, P], BF16)

                def hot_high_only(e, slot, cols):
                    e.tensor_tensor(hot_high[:, slot, :, :], column[:, 0:H].unsqueeze(1).to_broadcast([P, GROUP, H]),
                                    high[:, cols].unsqueeze(2).to_broadcast([P, GROUP, H]), ALU.is_equal)

                def hot_low_kept(e, slot, cols):
                    e.tensor_tensor(hot_low_late[:, slot, :, :], column[:, :].unsqueeze(1).to_broadcast([P, GROUP, P]),
                                    low[:, cols].unsqueeze(2).to_broadcast([P, GROUP, P]), ALU.is_equal)

                def scalar_table(s):
                    e = s.e
                    if s.live(1):
                        g2 = s.slot(1, 2)
                        for t in range(GROUP):
                            s.wait((s_step, lambda i, t=t: GROUP * (i - 1) + t), (s_look, done(3)))
                            e.activation(table[:, g2, t, :], bank[0][0:H, 0:P], ACT.Copy).then_inc(s_table.handle, 1)
                    if s.live(0):
                        g4 = s.slot(0, UNROLL)
                        s.wait((sp_scatter[g4], ring_count(UNROLL, UNROLL, 16 * GROUP)))
                        e.activation(load[:, g4, :, :].rearrange("p t w -> p (t w)"),
                                     words[:, :, :].rearrange("p k w -> p (k w)")[:, bass.ds(s.at(lambda i: 4 * GROUP * i), 4 * GROUP)],
                                     ACT.Copy).then_inc(s_load.handle, 1)

                def tensor_place(s):
                    e = s.e
                    if s.live(1):
                        g2, g4 = s.slot(1, 2), s.slot(1, UNROLL)
                        s.wait((s_place_hot, done(1)), (s_rank, done(3)))
                        for t in range(GROUP):
                            s.wait((s_table, lambda i, t=t: GROUP * (i - 1) + t + 1))
                            e.matmul(bank[0][0:H, 0:P], hot_high[:, g2, t, :], hot_low_late[:, g4, t, :],
                                     start=False, stop=True, skip_group_check=True).then_inc(s_step.handle, 1)
                            mm = e.matmul(bank[2 + g2][:, t * P:t * P + P], hot_rows[:, g2, t, :], table[:, g2, t, :], start=True, stop=True)
                        mm.then_inc(s_look.handle, 1)

                def pool_scatter(s):
                    if s.live(3):
                        g4 = s.slot(3, UNROLL)
                        s.wait((s_math, done(3, 4)), (s_load, done(3)), apart=True)
                        for t in range(GROUP):
                            s.e.indirect_dma_start(out=to, out_offset=bass.IndirectOffsetOnAxis(ap=place_to[:, g4, t:t + 1], axis=0),
                                                   in_=load[:, g4, t, :], in_offset=None).then_inc(sp_scatter[g4].handle, 16)

                with nc.Block() as block:
                    @block.sync
                    def _(e):
                        with if_unsorted(e, "sync"):
                            pipeline(e, f"{name}_ps", sync_rows, z.groups, UNROLL, (UNROLL,))

                    @block.vector
                    def _(e):
                        with if_unsorted(e, "vector"):
                            pipeline(e, f"{name}_pv", vector_place, z.groups, UNROLL + 2, (UNROLL, 16, 16 * GROUP))

                    @block.scalar
                    def _(e):
                        with if_unsorted(e, "scalar"):
                            pipeline(e, f"{name}_pa", scalar_table, z.groups, UNROLL, (UNROLL, GROUP * UNROLL, 16 * GROUP))

                    @block.tensor
                    def _(e):
                        with if_unsorted(e, "tensor"):
                            pipeline(e, f"{name}_pt", tensor_place, z.groups, UNROLL, (UNROLL, GROUP * UNROLL))

                    @block.gpsimd
                    def _(e):
                        with if_unsorted(e, "gpsimd"):
                            pipeline(e, f"{name}_pp", pool_scatter, z.groups, UNROLL, (UNROLL, GROUP * UNROLL))
                            for s in sp_scatter:
                                e.wait_ge(s.handle, s.base + 16 * z.tiles // UNROLL)

                if not often_sorted:
                    return
                in_rows = tensor(ctx, f"{name}_in_rows", [P, 3, z.tblocks, P], I32)
                as_float = tensor(ctx, f"{name}_as_float", [P, 3, z.tblocks, P])
                c = Chain(nc, sorted_count, sorted_pool_count, lambda e, engine: if_unsorted(e, engine, wanted=0))
                c.do("vector", lambda e: e.memset(in_rows[:, 0, :, :], 0))
                c.do("gpsimd", lambda e: e.memset(in_rows[:, 1, :, :], z.N))
                c.do("vector", lambda e: e.memset(in_rows[:, 2, :, :], 0))
                c.then()
                for w, array in enumerate((other_of, key_of, third_of)):
                    to_rows = in_rows[:, w, :, :] if w < 2 else in_rows[:, w, :, :].bitcast(third_dt)
                    blocks, left = divmod(z.E, P * P)
                    if blocks:
                        c.do("sync", lambda e, to_rows=to_rows, array=array: e.dma_start(
                            to_rows[:, 0:blocks, :], array[0:blocks * P * P].rearrange("(b t q) -> t b q", t=P, q=P)), dma=True)
                    lines, left = divmod(left, P)
                    start = blocks * P * P
                    if lines:
                        c.do("sync", lambda e, to_rows=to_rows, array=array: e.dma_start(
                            to_rows[0:lines, blocks, :], array[start:start + lines * P].rearrange("(t q) -> t q", q=P)), dma=True)
                    if left:
                        c.do("sync", lambda e, to_rows=to_rows, array=array: e.dma_start(
                            to_rows[lines:lines + 1, blocks, 0:left], array[start + lines * P:z.E].unsqueeze(0)), dma=True)
                c.then()
                for w in range(3):
                    c.do("vector", lambda e, w=w: e.tensor_copy(as_float[:, w, :, :], in_rows[:, w, :, :] if w < 2 else in_rows[:, w, :, :].bitcast(third_dt)))
                for w in range(3):
                    first_bank = w % 2 * (z.tblocks + GROUP - 1) // GROUP
                    c.then()
                    for b in range(z.tblocks):
                        c.do("tensor", lambda e, w=w, b=b, first_bank=first_bank: e.transpose(
                            bank[first_bank + b // GROUP][:, b % GROUP * P:b % GROUP * P + P], as_float[:, w, b, :], ident[:, :]))
                    c.then()
                    for b in range(0, z.tblocks, GROUP):
                        n = min(GROUP * P, z.tiles - b * P)
                        engine = "vector" if b % (2 * GROUP) else "scalar"
                        c.do(engine, copy(words[:, b * P:b * P + n, w], bank[first_bank + b // GROUP][:, 0:n], engine))
                c.then()
                c.do("sync", lambda e: e.dma_start(to.rearrange("(p k) w -> p k w", p=P), words[:, :, :]), dma=True)
                c.run()

        def layout(ctx, name, of, third_rows):
            others = tensor(ctx, f"{name}_others", [P, z.tiles], I32)
            weights = None if third_rows else tensor(ctx, f"{name}_weights", [P, z.tiles])
            q0 = tensor(ctx, f"{name}_q0", [1, z.tblocks * P], I32)
            cnt = tensor(ctx, f"{name}_cnt", [P, z.ntiles])
            last_run = tensor(ctx, f"{name}_last_run", [P, z.ntiles], I32)
            run_col = None if not third_rows else tensor(ctx, f"{name}_run_col", [P, z.rblocks], I32)
            within = None if third_rows else tensor(ctx, f"{name}_within", [P, z.tblocks * P])
            go_on = None if third_rows else tensor(ctx, f"{name}_go_on", [P, z.R], BF16)
            with ExitStack() as tmp:
                go_on = go_on or tensor(tmp, f"{name}_go_on", [P, z.R], BF16)
                words = tensor(tmp, f"{name}_sorted", [P, z.tiles, 4])
                col = tensor(tmp, f"{name}_col", [P, z.tblocks * P])
                turned = tensor(tmp, f"{name}_kt", [P, z.tblocks, P])
                flag = tensor(tmp, f"{name}_flag", [P, z.tblocks, P])
                inner = tensor(tmp, f"{name}_inner", [P, z.tblocks, P])
                number = tensor(tmp, f"{name}_number", [P, z.tblocks, P])
                half = tensor(tmp, f"{name}_half", [P, z.tblocks, 2, P], BF16)
                per = tensor(tmp, f"{name}_per", [P, z.tblocks])
                tot = tensor(tmp, f"{name}_tot", [P, z.tblocks])
                acc = tensor(tmp, f"{name}_acc", [P, z.tblocks])
                qi = tensor(tmp, f"{name}_qi", [P, z.tblocks], I32)
                node = tensor(tmp, f"{name}_node", [P, z.ntiles])
                nf = tensor(tmp, f"{name}_nf", [P, 2, z.ntiles])
                start_run = tensor(tmp, f"{name}_start_run", [P, z.ntiles], I32)
                minus = tensor(tmp, f"{name}_minus", [P, z.RW // P])
                keys = tensor(tmp, f"{name}_keys", [P, z.R])
                keyi = tensor(tmp, f"{name}_keyi", [1, z.R], I32)
                c = chain()
                c.do("sync", lambda e: e.dma_start(words[:, :, :], of.rearrange("(p k) w -> p k w", p=P)), dma=True)
                c.do("vector", lambda e: e.memset(col[:, :], float(z.N)))
                c.do("vector", lambda e: e.memset(inner[:, :, :], 1.0))
                c.do("vector", lambda e: e.memset(minus[:, :], -1.0))
                c.do("gpsimd", lambda e: e.iota(node[:, :], [[1, z.ntiles]], base=0, channel_multiplier=z.ntiles,
                                                allow_small_or_imprecise_dtypes=True))
                flat = node_words.rearrange("w a b -> w (a b)")
                c.do("sync", lambda e: e.dma_start(cnt[:, :], flat[0, 0:z.NP].rearrange("(p t) -> p t", p=P)), dma=True)
                c.do("sync", lambda e: e.dma_start(nf[:, :, :], flat[1:3, 0:z.NP].rearrange("w (p t) -> p w t", p=P)), dma=True)
                c.then()
                c.do("sync", lambda e: e.dma_start(run_keys.rearrange("(p k) w -> p (k w)", p=P), minus[:, :]), dma=True)
                c.do("vector", lambda e: e.tensor_copy(start_run[:, :], nf[:, 0, :]))
                c.do("vector", lambda e: e.tensor_copy(last_run[:, :], nf[:, 1, :]))
                c.do("vector", lambda e: e.tensor_copy(col[:, 0:z.tiles], words[:, :, 1]))
                c.do("vector", lambda e: e.tensor_copy(others[:, :], words[:, :, 0]))
                if not third_rows:
                    c.do("vector", lambda e: e.tensor_copy(weights[:, :], words[:, :, 2]))
                c.do("gpsimd", lambda e: e.memset(inner[:, :, 0:1], 0.0))
                rows_of(c, col, z.tblocks, turned)
                for t in range(z.ntiles):
                    c.do("gpsimd", lambda e, t=t: e.indirect_dma_start(
                        out=run_keys, out_offset=bass.IndirectOffsetOnAxis(ap=start_run[:, t:t + 1], axis=0),
                        in_=node[:, t:t + 1], in_offset=None, bounds_check=z.RW - 1, oob_is_err=False), dma=True)
                c.then()
                c.do("vector", lambda e: e.memset(flag[:, :, 0:1], 1.0))
                c.do("vector", lambda e: e.tensor_tensor(flag[:, :, 1:P], turned[:, :, 1:P], turned[:, :, 0:P - 1], ALU.not_equal))
                c.do("sync", lambda e: e.dma_start(keys[:, :], run_keys.rearrange("r w -> (r w)")[0:z.R].partition_broadcast(P)), dma=True)
                c.then()
                c.do("vector", lambda e: e.tensor_tensor_scan(number[:, :, :].rearrange("p b q -> p (b q)"),
                                                              inner[:, :, :].rearrange("p b q -> p (b q)"),
                                                              flag[:, :, :].rearrange("p b q -> p (b q)"), 0.0, ALU.mult, ALU.add))
                c.do("vector", lambda e: e.tensor_scalar(go_on[:, :], keys[:, :], 0.0, None, ALU.is_lt))
                c.then()
                c.do("vector", lambda e: e.tensor_copy(per[:, :], number[:, :, P - 1]))
                c.then()
                c.do("tensor", lambda e: e.matmul(bank[4][:, 0:z.tblocks], above[:, :], per[:, :], start=True, stop=True))
                c.do("tensor", lambda e: e.matmul(bank[5][:, 0:z.tblocks], ones[:, :], per[:, :], start=True, stop=True))
                c.do("vector", lambda e: e.tensor_scalar(number[:, :, :], number[:, :, :], -1.0, None, ALU.add))
                c.then()
                c.do("vector", lambda e: e.tensor_copy(tot[:, :], bank[5][:, 0:z.tblocks]))
                c.do("vector", lambda e: e.tensor_copy(half[:, :, 1, :], number[:, :, :]))
                c.then()
                c.do("vector", lambda e: e.tensor_tensor_scan(acc[:, :], ones[:, 0:z.tblocks], tot[:, :], 0.0, ALU.mult, ALU.add))
                c.then()
                c.do("vector", lambda e: e.tensor_tensor(acc[:, :], acc[:, :], tot[:, :], ALU.subtract))
                c.then()
                c.do("vector", lambda e: e.tensor_tensor(qi[:, :], acc[:, :], bank[4][:, 0:z.tblocks], ALU.add))
                c.then()
                c.do("sync", lambda e: e.dma_start(first_run.rearrange("(b t) -> t b", t=P), qi[:, :], allow_slow_non_contiguous=True), dma=True)
                c.then()
                c.do("sync", lambda e: e.dma_start(q0[:, :], first_run.unsqueeze(0)), dma=True)
                if third_rows:
                    c.do("vector", lambda e: e.memset(col[:, :], 0.0))
                    c.do("vector", lambda e: e.tensor_tensor_scan(keys[0:1, :], keys[0:1, :], keys[0:1, :], -1.0, ALU.max, ALU.max))
                    c.then()
                    c.do("vector", lambda e: e.tensor_copy(col[:, 0:z.tiles], words[:, :, 2]))
                    c.do("vector", lambda e: e.tensor_copy(keyi[:, :], keys[0:1, :]))
                    rows_of(c, col, z.tblocks, turned)
                    c.then()
                    c.do("vector", lambda e: e.tensor_copy(half[:, :, 0, :], turned[:, :, :]))
                    c.do("sync", lambda e: e.dma_start(run_node.unsqueeze(0), keyi[:, :]), dma=True)
                    c.do("sync", lambda e: e.dma_start(run_goes_on.unsqueeze(0), go_on[0:1, :]), dma=True)
                    c.then()
                    c.do("sync", lambda e: e.dma_start(tile_rows.rearrange("(b t) w p -> t b w p", t=P), half[:, :, :, :]), dma=True)
                    c.do("sync", lambda e: e.dma_start(run_col[:, :], run_node.rearrange("(b r) -> r b", r=P), allow_slow_non_contiguous=True), dma=True)
                else:
                    c.then()
                    for b in range(z.tblocks):
                        c.do("tensor", lambda e, b=b: e.transpose(bank[b // GROUP][:, b % GROUP * P:b % GROUP * P + P], number[:, b, :], ident[:, :]))
                    c.then()
                    for b in range(0, z.tblocks, GROUP):
                        n = min(GROUP, z.tblocks - b)
                        c.do("vector", copy(within[:, b * P:(b + n) * P], bank[b // GROUP][:, 0:n * P], "vector"))
                c.run()
            return others, weights, q0, cnt, last_run, go_on, run_col, within

        def load_q0(s, e_type, q0, lag):
            _, values = nc.values_load_multi_w_load_instructions(
                q0[0:1, bass.ds(s.at(lambda i: GROUP * (i - lag)), GROUP)], engines=[e_type],
                min_val=0, max_val=z.R, skip_runtime_bounds_check_because="a prefix sum of run counts")
            return values

        def to_nodes(c, table, last_run, rows_sb, node):
            c.do("gpsimd", lambda e: e.memset(node[:, :, :], 0.0))
            per_round = 4 * GROUP
            for r in range(0, z.rblocks, per_round):
                n = min(per_round, z.rblocks - r)
                c.then()
                for b in range(n):
                    c.do("tensor", lambda e, b=b, r=r: e.transpose(bank[b // GROUP][:, b % GROUP * P:b % GROUP * P + P],
                                                                   table[:, (r + b) * P:(r + b) * P + P], ident[:, :]))
                c.then()
                for b in range(0, n, GROUP):
                    m = min(GROUP, n - b)
                    engine = "vector" if b % (2 * GROUP) else "scalar"
                    c.do(engine, copy(rows_sb[:, b:b + m, :], bank[b // GROUP][:, 0:m * P].rearrange("p (b q) -> p b q", b=m), engine))
                c.then()
                c.do("sync", lambda e, r=r, n=n: e.dma_start(run_out.rearrange("(b q) d -> q b d", q=P)[:, r:r + n, :], rows_sb[:, 0:n, :]), dma=True)
            c.then()
            for t in range(z.ntiles):
                c.do("gpsimd", lambda e, t=t: e.indirect_dma_start(
                    out=node[:, t, :], out_offset=None, in_=run_out,
                    in_offset=bass.IndirectOffsetOnAxis(ap=last_run[:, t:t + 1], axis=0),
                    bounds_check=z.R - 1, oob_is_err=False), dma=True)

        def layer_norm(c, v, tmp, col, eps):
            def wide(a):
                return a.unsqueeze(2).to_broadcast([P, z.ntiles, z.D])
            c.then()
            c.do("vector", lambda e: e.tensor_reduce(col[:, :], v[:, :, :], AX_X, ALU.add))
            c.then()
            c.do("vector", lambda e: e.tensor_scalar(col[:, :], col[:, :], 1.0 / z.D, None, ALU.mult))
            c.then()
            c.do("vector", lambda e: e.tensor_tensor(v[:, :, :], v[:, :, :], wide(col[:, :]), ALU.subtract))
            c.then()
            c.do("vector", lambda e: e.tensor_tensor(tmp[:, :, :], v[:, :, :], v[:, :, :], ALU.mult))
            c.then()
            c.do("vector", lambda e: e.tensor_reduce(col[:, :], tmp[:, :, :], AX_X, ALU.add))
            c.then()
            c.do("vector", lambda e: e.tensor_scalar(col[:, :], col[:, :], 1.0 / z.D, eps, ALU.mult, ALU.add))
            c.then()
            c.do("scalar", lambda e: e.activation(col[:, :], col[:, :], ACT.Sqrt))
            c.then()
            c.do("vector", lambda e: e.reciprocal(col[:, :], col[:, :]))
            c.then()
            c.do("vector", lambda e: e.tensor_tensor(v[:, :, :], v[:, :, :], wide(col[:, :]), ALU.mult))

        sort_edges("d", dst, src, edge_weight, F32, by_dst, often_sorted=True)
        whole = z.N // z.ntiles
        odd = z.N - whole * z.ntiles
        with ExitStack() as ctx:
            others, weights, q0, cnt, last_run, go_on, _, within = layout(ctx, "l0", by_dst, False)
            table = tensor(ctx, "l0_table", [P, z.RW])
            nodes = tensor(ctx, "nodes", [P, z.ntiles, z.D])
            idx = tensor(ctx, "l0_idx", [P, UNROLL, GROUP], I32)
            rows = tensor(ctx, "l0_rows", [P, UNROLL, GROUP, z.D])
            spread = tensor(ctx, "l0_spread", [P, 2, GROUP, P])
            w1_sb, w2_sb = tensor(ctx, "w1_sb", [P, P]), tensor(ctx, "w2_sb", [P, P])
            b1_sb, b2_sb = tensor(ctx, "b1_sb", [P, 1]), tensor(ctx, "b2_sb", [P, P])
            c = chain()
            c.do("vector", lambda e: e.memset(table[:, :], 0.0))
            c.do("gpsimd", lambda e: e.memset(nodes[:, :, :], 0.0))
            c.then()
            c.do("sync", lambda e: e.dma_start(nodes[0:whole, :, :], x[0:whole * z.ntiles, :].rearrange("(p t) d -> p t d", t=z.ntiles)), dma=True)
            if odd:
                c.do("sync", lambda e: e.dma_start(nodes[whole:whole + 1, 0:odd, :], x[whole * z.ntiles:z.N, :].unsqueeze(0)), dma=True)
            for sb, a in ((w1_sb[:, :], w1), (w2_sb[:, :], w2), (b1_sb[:, :], b1.unsqueeze(1)), (b2_sb[:, :], b2.partition_broadcast(P))):
                c.do("scalar", lambda e, sb=sb, a=a: e.dma_start(sb, a), dma=True)
            c.run()

            def pool_gather(idx, rows, table_rows, s_free):
                def program(s):
                    if s.live(0):
                        g4 = s.slot(0, UNROLL)
                        s.wait((s_free, done(UNROLL)), (s_copy_idx, done(0)), apart=True)
                        for t in range(GROUP):
                            s.e.indirect_dma_start(out=rows[:, g4, t, :], out_offset=None, in_=table_rows,
                                                   in_offset=bass.IndirectOffsetOnAxis(ap=idx[:, g4, t:t + 1], axis=0))\
                                .then_inc(sp_gather[g4].handle, 16)
                return program

            def copy_idx(s, idx, s_free):
                if s.live(0):
                    s.wait((s_free, done(UNROLL)))
                    s.e.activation(idx[:, s.slot(0, UNROLL), :], others[:, bass.ds(s.at(lambda i: GROUP * i), GROUP)], ACT.Copy)\
                        .then_inc(s_copy_idx.handle, 1)

            def vector_l0(s):
                e = s.e
                if s.live(3):
                    q = load_q0(s, mybir.EngineType.DVE, q0, 3)
                if s.live(0):
                    s.wait((s_mm, done(2)))
                    for t in range(GROUP):
                        col = bass.ds(s.at(lambda i, t=t: GROUP * i + t), 1)
                        last = e.tensor_scalar(spread[:, s.slot(0, 2), t, :], column[:, :], within[:, col],
                                               weights[:, col], ALU.is_equal, ALU.mult)
                    last.then_inc(s_weights.handle, 1)
                if s.live(3):
                    for t in range(GROUP):
                        s.wait((s_mm, done(3)), (s_write, lambda i, t=t: GROUP * (i - 3) + t))
                        e.tensor_copy(table[:, bass.ds(q[t], P)], bank[s.slot(3, 2)][:, t * P:t * P + P]).then_inc(s_write.handle, 1)

            def tensor_l0(s):
                if s.live(2):
                    s.wait((s_weights, done(2)), (sp_gather[s.slot(2, UNROLL)], ring_count(2, UNROLL, 16 * GROUP)), (s_write, done(4, GROUP)))
                    for t in range(GROUP):
                        mm = s.e.matmul(bank[s.slot(2, 2)][:, t * P:t * P + P], rows[:, s.slot(2, UNROLL), t, :], spread[:, s.slot(2, 2), t, :],
                                        start=True, stop=True)
                    mm.then_inc(s_mm.handle, 1)

            with nc.Block() as block:
                @block.gpsimd
                def _(e):
                    pipeline(e, "gp", pool_gather(idx, rows, x, s_mm), z.groups, UNROLL, (UNROLL,))

                @block.scalar
                def _(e):
                    pipeline(e, "ga", lambda s: copy_idx(s, idx, s_mm), z.groups, UNROLL, (UNROLL,))

                @block.vector
                def _(e):
                    pipeline(e, "gv", vector_l0, z.groups, UNROLL, (UNROLL, GROUP * UNROLL))

                @block.tensor
                def _(e):
                    pipeline(e, "gt", tensor_l0, z.groups, UNROLL + 1, (UNROLL, 16 * GROUP, GROUP * UNROLL))
            for s in (s_copy_idx, s_mm, s_weights):
                s.base += z.groups
            s_write.base += z.tiles
            for s in sp_gather:
                s.base += 16 * z.tiles // UNROLL

            agg = tensor(ctx, "l0_agg", [P, z.ntiles, z.D])
            rows_sb = tensor(ctx, "l0_rows_sb", [P, 4 * GROUP, P])
            c = chain()
            c.do("vector", lambda e: e.tensor_tensor_scan(table[:, 0:z.R], go_on[:, :], table[:, 0:z.R], 0.0, ALU.mult, ALU.add))
            to_nodes(c, table, last_run, rows_sb, agg)
            c.then()
            c.do("vector", lambda e: e.tensor_tensor(agg[:, :, :], agg[:, :, :], nodes[:, :, :], ALU.add))
            c.then()
            c.do("gpsimd", lambda e: e.tensor_tensor(nodes[:, :, :], nodes[:, :, :], b2_sb[:, :].unsqueeze(1).to_broadcast([P, z.ntiles, z.D]), ALU.add))
            turned = tensor(ctx, "l0_turned", [P, BANK])
            hidden = tensor(ctx, "l0_hidden", [P, BANK])
            for r in range(0, z.ntiles, GROUP):
                n = min(GROUP, z.ntiles - r)
                c.then()
                for t in range(n):
                    c.do("tensor", lambda e, r=r, t=t: e.transpose(bank[0][:, t * P:t * P + P], agg[:, r + t, :], ident[:, :]))
                c.then()
                c.do("scalar", lambda e, n=n: e.activation(turned[:, 0:n * P], bank[0][:, 0:n * P], ACT.Copy))
                c.then()
                c.do("tensor", lambda e, n=n: e.matmul(bank[1][:, 0:n * P], w1_sb[:, :], turned[:, 0:n * P], start=True, stop=True))
                c.then()
                c.do("scalar", lambda e, n=n: e.activation(hidden[:, 0:n * P], bank[1][:, 0:n * P], ACT.Relu, bias=b1_sb[:, 0:1]))
                c.then()
                for t in range(n):
                    c.do("tensor", lambda e, t=t: e.matmul(bank[2][:, t * P:t * P + P], hidden[:, t * P:t * P + P], w2_sb[:, :], start=True, stop=True))
                c.then()
                c.do("vector", lambda e, r=r, n=n: e.tensor_tensor(nodes[:, r:r + n, :], nodes[:, r:r + n, :],
                                                                   bank[2][:, 0:n * P].rearrange("p (t d) -> p t d", t=n), ALU.add))
            col49 = tensor(ctx, "l0_col49", [P, z.ntiles])
            layer_norm(c, nodes, agg, col49, LN_EPS)
            c.then()
            for to in (node_rows, entity_rows):
                c.do("sync", lambda e, to=to: e.dma_start(to.rearrange("(p t) d -> p t d", p=P), nodes[:, :, :]), dma=True)
            if debug is not None and "x1" in debug:
                c.do("sync", lambda e: e.dma_start(debug["x1"].rearrange("(p t) d -> p t d", p=P), nodes[:, :, :]), dma=True)
            c.run()

        sort_edges("s", src, dst, edge_type, I32, by_src)
        others, _, q0, cnt, last_run, _, run_col, _ = layout(top, "l1", by_src, True)
        per_edge = tensor(top, "per_edge", [P, z.ntiles])
        result = tensor(top, "result", [P, z.ntiles, z.D])
        q_sb, k_sb = tensor(top, "q_sb", [P, P]), tensor(top, "k_sb", [P, P])
        emb_hi_mid = tensor(top, "emb_hi_mid", [P, z.D], BF16)
        emb_lo = tensor(top, "emb_lo", [z.T, z.D], BF16)
        with ExitStack() as ctx:
            emb = tensor(ctx, "emb", [P, z.D])
            hi = tensor(ctx, "hi", [P, z.D], BF16)
            left = tensor(ctx, "left", [P, z.D])
            mid = tensor(ctx, "mid", [P, z.D], BF16)
            c = chain()
            c.do("vector", lambda e: e.memset(result[:, :, :], 0.0))
            c.do("sync", lambda e: e.dma_start(q_sb[:, :], q_w), dma=True)
            c.do("sync", lambda e: e.dma_start(k_sb[:, :], k_w), dma=True)
            c.do("sync", lambda e: e.dma_start(emb[0:z.T, :], edge_emb), dma=True)
            c.do("sync", lambda e: e.dma_start(emb[z.T:P, :], edge_emb), dma=True)
            c.then()
            c.do("vector", lambda e: e.tensor_copy(hi[:, :], emb[:, :]))
            c.do("vector", lambda e: e.tensor_scalar(cnt[:, :], cnt[:, :], 1.0, None, ALU.max))
            c.then()
            c.do("vector", lambda e: e.tensor_tensor(left[:, :], emb[:, :], hi[:, :], ALU.subtract))
            c.do("vector", lambda e: e.reciprocal(per_edge[:, :], cnt[:, :]))
            c.then()
            c.do("vector", lambda e: e.tensor_copy(mid[:, :], left[:, :]))
            c.then()
            c.do("vector", lambda e: e.tensor_copy(emb_hi_mid[0:z.T, :], hi[0:z.T, :]))
            c.do("vector", lambda e: e.tensor_copy(emb_hi_mid[z.T:P, :], mid[z.T:P, :]))
            c.do("vector", lambda e: e.tensor_tensor(emb_lo[:, :], left[0:z.T, :], mid[0:z.T, :], ALU.subtract))
            c.run()

        s_row = [sem(f"s_row{i}") for i in range(UNROLL)]
        s_win = [sem(f"s_win{i}") for i in range(UNROLL)]
        s_oht, s_rel, s_rt, s_rtt, s_rts = sem("s_oht"), sem("s_rel"), sem("s_rt"), sem("s_rtt"), sem("s_rts")
        s_kw, s_th, s_att, s_min, s_exp = sem("s_kw"), sem("s_th"), sem("s_att"), sem("s_min"), sem("s_exp")
        s_et, s_ets, s_acc, s_stat = sem("s_et"), sem("s_ets"), sem("s_acc"), sem("s_stat")
        trows = tile_rows.rearrange("t w p -> (t w p)")

        for hop in range(HOPS):
            with ExitStack() as ctx:
                table = tensor(ctx, f"table{hop}", [P, z.RW])
                stats = tensor(ctx, f"stats{hop}", [2, z.RW])
                with ExitStack() as inner:
                    qt = tensor(inner, f"qt{hop}", [P, z.RW])
                    with ExitStack() as tmp:
                        heads = tensor(tmp, f"heads{hop}", [P, 2, 4 * GROUP, z.D])
                        turned = tensor(tmp, f"headt{hop}", [P, GROUP, BANK])
                        c = chain()
                        c.do("vector", lambda e: e.memset(qt[:, z.R:z.RW], 0.0))

                        def gather_heads(r):
                            for b in range(r, min(r + 4 * GROUP, z.rblocks)):
                                c.do("gpsimd", lambda e, b=b: e.indirect_dma_start(
                                    out=heads[:, b // (4 * GROUP) % 2, b % (4 * GROUP), :], out_offset=None, in_=node_rows,
                                    in_offset=bass.IndirectOffsetOnAxis(ap=run_col[:, b:b + 1], axis=0)), dma=True)

                        gather_heads(0)
                        c.do("vector", lambda e: e.memset(table[:, :], 0.0))
                        c.do("vector", lambda e: e.memset(stats[:, :], 1.0))
                        for r in range(0, z.rblocks, 4 * GROUP):
                            n = min(4 * GROUP, z.rblocks - r)
                            c.then()
                            gather_heads(r + 4 * GROUP)
                            for b in range(n):
                                c.do("tensor", lambda e, b=b, r=r: e.transpose(bank[b // GROUP][:, b % GROUP * P:b % GROUP * P + P], heads[:, r // (4 * GROUP) % 2, b, :], ident[:, :]))
                            c.then()
                            banks = [(k, min(GROUP, n - k * GROUP) * P) for k in range(ceil(n / GROUP))]
                            for k, w in banks:
                                engine = "vector" if k % 2 else "scalar"
                                c.do(engine, copy(turned[:, k, 0:w], bank[k][:, 0:w], engine))
                            c.then()
                            for k, w in banks:
                                c.do("tensor", lambda e, k=k, w=w: e.matmul(bank[4 + k][:, 0:w], q_sb[:, :], turned[:, k, 0:w], start=True, stop=True))
                            c.then()
                            for k, w in banks:
                                engine = "vector" if k % 2 else "scalar"
                                c.do(engine, copy(qt[:, r * P + k * BANK:r * P + k * BANK + w], bank[4 + k][:, 0:w], engine, scale=-1.0))
                        c.run()

                    idx = tensor(inner, f"idx{hop}", [P, UNROLL, GROUP], I32)
                    tails = tensor(inner, f"tails{hop}", [P, UNROLL, GROUP, z.D])
                    rows_in = tensor(inner, f"rows_in{hop}", [P, UNROLL, GROUP, 2, P], BF16)
                    window = tensor(inner, f"window{hop}", [P, UNROLL, GROUP, P])
                    hot_type = tensor(inner, f"hot_type{hop}", [P, 2, GROUP, P], BF16)
                    mask = tensor(inner, f"mask{hop}", [P, UNROLL, GROUP, P], BF16)
                    rt = tensor(inner, f"rt{hop}", [P, UNROLL, GROUP, z.D])
                    rtt = tensor(inner, f"rtt{hop}", [P, 2, BANK])
                    right = tensor(inner, f"right{hop}", [P, 2, BANK])
                    att = tensor(inner, f"att{hop}", [P, 2, GROUP, P])
                    stat = tensor(inner, f"stat{hop}", [P, 2, GROUP, 2])
                    weight = tensor(inner, f"weight{hop}", [P, 2, GROUP, P])
                    weight_t = tensor(inner, f"weight_t{hop}", [P, 2, GROUP, P])
                    b_rel, b_rtt, b_kw, b_att, b_et, b_acc = range(6)
                    b_st = (6, 7)

                    def sync_hop(s):
                        if not s.live(0):
                            return
                        g4 = s.slot(0, UNROLL)
                        at = s.at(lambda i: GROUP * 2 * P * i)
                        q = load_q0(s, mybir.EngineType.SP, q0, 0)
                        s.wait((s_oht, done(UNROLL)))
                        s.e.dma_start(rows_in[:, g4, :, :, :].rearrange("q t w p -> q (t w p)"),
                                      trows[bass.ds(at, GROUP * 2 * P)].partition_broadcast(P)).then_inc(s_row[g4].handle, 16)
                        s.wait((s_att, done(UNROLL)))
                        for t in range(GROUP):
                            s.e.dma_start(window[:, g4, t, :], qt[:, bass.ds(q[t], P)]).then_inc(s_win[g4].handle, 16)

                    def vector_hop(s):
                        e = s.e
                        if s.live(5):
                            q = load_q0(s, mybir.EngineType.DVE, q0, 5)
                            s.wait((s_acc, done(5)))
                            for t in range(GROUP):
                                s.wait((s_write, lambda i, t=t: GROUP * (i - 5) + t))
                                e.tensor_copy(table[:, bass.ds(q[t], P)], bank[b_acc][:, t * P:t * P + P]).then_inc(s_write.handle, 1)
                                s.wait((s_stat, lambda i, t=t: GROUP * (i - 5) + t))
                                e.tensor_copy(stats[:, bass.ds(q[t], P)], bank[b_st[s.slot(5, 2)]][0:2, t * P:t * P + P]).then_inc(s_stat.handle, 1)
                        if s.live(1):
                            g4 = s.slot(1, UNROLL)
                            s.wait((s_rel, done(1)), (sp_gather[g4], ring_count(1, UNROLL, 16 * GROUP)))
                            e.tensor_tensor(rt[:, g4, :, :].rearrange("p t d -> p (t d)"), bank[b_rel][:, :],
                                            tails[:, g4, :, :].rearrange("p t d -> p (t d)"), ALU.mult).then_inc(s_rt.handle, 1)
                        if s.live(3):
                            g2, g4 = s.slot(3, 2), s.slot(3, UNROLL)
                            s.wait((s_att, done(3)), apart=True)
                            for t in range(GROUP):
                                e.tensor_tensor_reduce(att[:, g2, t, :], bank[b_att][:, t * P:t * P + P], mask[:, g4, t, :],
                                                       1.0, START, ALU.add, ALU.min, stat[:, g2, t, 0:1]).then_inc(s_min.handle, 1)
                        if s.live(0):
                            g2, g4 = s.slot(0, 2), s.slot(0, UNROLL)
                            s.wait((s_row[g4], ring_count(0, UNROLL, 16)), (s_rel, done(2)), (s_min, done(4, GROUP)))
                            e.tensor_scalar(hot_type[:, g2, :, :], rows_in[:, g4, :, 0, :], row_half[:, 0:1], None, ALU.is_equal)
                            e.tensor_scalar(mask[:, g4, :, :], rows_in[:, g4, :, 1, :], row[:, 0:1], BIG, ALU.not_equal, ALU.mult)\
                                .then_inc(s_oht.handle, 1)

                    def tensor_hop(s):
                        e = s.e
                        if s.live(1):
                            g2 = s.slot(1, 2)
                            s.wait((s_oht, done(1)), (s_rt, done(2)))
                            for t in range(GROUP):
                                e.matmul(bank[b_rel][:, t * P:t * P + P], hot_type[:, g2, t, :], emb_hi_mid[:, :], start=True, stop=False)
                                mm = e.matmul(bank[b_rel][:, t * P:t * P + P], hot_type[0:z.T, g2, t, :], emb_lo[:, :], start=False, stop=True)
                            mm.then_inc(s_rel.handle, 1)
                        if s.live(3):
                            g2, g4 = s.slot(3, 2), s.slot(3, UNROLL)
                            s.wait((s_th, done(3)), (s_win[g4], ring_count(3, UNROLL, 16 * GROUP)), (s_min, done(4, GROUP)))
                            for t in range(GROUP):
                                mm = e.matmul(bank[b_att][:, t * P:t * P + P], window[:, g4, t, :], right[:, g2, t * P:t * P + P], start=True, stop=True)
                            mm.then_inc(s_att.handle, 1)
                        if s.live(4):
                            g2 = s.slot(4, 2)
                            s.wait((s_exp, done(4, GROUP)), (s_ets, done(5)), (s_stat, done(6, GROUP)))
                            for t in range(GROUP):
                                e.transpose(bank[b_et][:, t * P:t * P + P], weight[:, g2, t, :], ident[:, :])
                                mm = e.transpose(bank[b_st[g2]][0:2, t * P:t * P + P], stat[:, g2, t, :], ident[:, :])
                            mm.then_inc(s_et.handle, 1)
                        if s.live(2):
                            s.wait((s_rts, done(2)), (s_th, done(3)))
                            e.matmul(bank[b_kw][:, :], k_sb[:, :], rtt[:, s.slot(2, 2), :], start=True, stop=True).then_inc(s_kw.handle, 1)
                        if s.live(1):
                            s.wait((s_rt, done(1)), (s_rts, done(2)))
                            for t in range(GROUP):
                                mm = e.transpose(bank[b_rtt][:, t * P:t * P + P], rt[:, s.slot(1, UNROLL), t, :], ident[:, :])
                            mm.then_inc(s_rtt.handle, 1)
                        if s.live(4):
                            s.wait((s_ets, done(4)), (s_write, done(5, GROUP)))
                            for t in range(GROUP):
                                mm = e.matmul(bank[b_acc][:, t * P:t * P + P], rt[:, s.slot(4, UNROLL), t, :], weight_t[:, s.slot(4, 2), t, :],
                                              start=True, stop=True)
                            mm.then_inc(s_acc.handle, 1)

                    def scalar_hop(s):
                        e = s.e
                        copy_idx(s, idx, s_rt)
                        if s.live(4):
                            s.wait((s_et, done(4)), (s_acc, done(6)))
                            e.activation(weight_t[:, s.slot(4, 2), :, :].rearrange("p t d -> p (t d)"), bank[b_et][:, :], ACT.Copy).then_inc(s_ets.handle, 1)
                        if s.live(2):
                            s.wait((s_kw, done(2)))
                            e.activation(right[:, s.slot(2, 2), :], bank[b_kw][:, :], ACT.Tanh).then_inc(s_th.handle, 1)
                        if s.live(1):
                            s.wait((s_rtt, done(1)))
                            e.activation(rtt[:, s.slot(1, 2), :], bank[b_rtt][:, :], ACT.Copy).then_inc(s_rts.handle, 1)
                        if s.live(3):
                            g2 = s.slot(3, 2)
                            for t in range(GROUP):
                                s.wait((s_min, lambda i, t=t: GROUP * (i - 3) + t + 1))
                                e.activation(weight[:, g2, t, :], att[:, g2, t, :], ACT.Exp, scale=-1.0, bias=stat[:, g2, t, 0:1],
                                             accum_out=stat[:, g2, t, 1:2]).then_inc(s_exp.handle, 1)

                    deep = 2 * UNROLL
                    with nc.Block() as block:
                        @block.sync
                        def _(e):
                            pipeline(e, f"hs{hop}", sync_hop, z.groups, deep, (UNROLL,))

                        @block.gpsimd
                        def _(e):
                            pipeline(e, f"hp{hop}", pool_gather(idx, tails, node_rows, s_rt), z.groups, deep, (UNROLL,))

                        @block.vector
                        def _(e):
                            pipeline(e, f"hd{hop}", vector_hop, z.groups, deep, (UNROLL, GROUP * UNROLL, 16 * GROUP))

                        @block.tensor
                        def _(e):
                            pipeline(e, f"he{hop}", tensor_hop, z.groups, deep, (UNROLL, GROUP * UNROLL, 16 * GROUP))

                        @block.scalar
                        def _(e):
                            pipeline(e, f"ha{hop}", scalar_hop, z.groups, deep, (UNROLL, GROUP * UNROLL))
                    for s in (s_copy_idx, s_oht, s_rel, s_rt, s_rtt, s_rts, s_kw, s_th, s_att, s_et, s_ets, s_acc):
                        s.base += z.groups
                    for s in (s_write, s_stat, s_min, s_exp):
                        s.base += z.tiles
                    for s in s_row:
                        s.base += 16 * z.groups // UNROLL
                    for s in (*s_win, *sp_gather):
                        s.base += 16 * z.tiles // UNROLL

                with ExitStack() as tmp:
                    parts = 4
                    C = z.R // parts
                    low = tensor(tmp, f"low{hop}", [P, C])
                    total = tensor(tmp, f"total{hop}", [P, C])
                    least = tensor(tmp, f"least{hop}", [P, C + 1])
                    fade = tensor(tmp, f"fade{hop}", [P, C])
                    gain = tensor(tmp, f"gain{hop}", [P, C])
                    apart = tensor(tmp, f"apart{hop}", [P, C])
                    go_on = tensor(tmp, f"go_on{hop}", [P, C], BF16)
                    carry = tensor(tmp, f"carry{hop}", [P, 1])
                    c = chain()
                    c.do("sync", lambda e: e.dma_start(run_stats, stats[:, :]), dma=True)
                    c.do("vector", lambda e: e.memset(least[:, 0:1], BIG))
                    c.do("vector", lambda e: e.memset(carry[:, :], 0.0))
                    for r in range(parts):
                        cols = slice(r * C, r * C + C)
                        c.then()
                        c.do("sync", lambda e, cols=cols: e.dma_start(low[:, :], run_stats[0, cols].partition_broadcast(P)), dma=True)
                        c.do("sync", lambda e, cols=cols: e.dma_start(total[:, :], run_stats[1, cols].partition_broadcast(P)), dma=True)
                        c.do("scalar", lambda e, cols=cols: e.dma_start(go_on[:, :], run_goes_on[cols].partition_broadcast(P)), dma=True)
                        c.then()
                        c.do("vector", lambda e: e.tensor_scalar(apart[:, :], go_on[:, :], -BIG, BIG, ALU.mult, ALU.add))
                        c.then()
                        c.do("vector", lambda e: e.tensor_tensor_scan(least[:, 1:], apart[:, :], low[:, :], least[:, 0:1], ALU.add, ALU.min))
                        c.then()
                        c.do("vector", lambda e: e.tensor_tensor(gain[:, :], least[:, 1:], low[:, :], ALU.subtract))
                        c.do("vector", lambda e: e.tensor_tensor(fade[:, :], least[:, 1:], least[:, 0:C], ALU.subtract))
                        c.then()
                        c.do("scalar", lambda e: e.activation(gain[:, :], gain[:, :], ACT.Exp))
                        c.do("vector", lambda e: e.tensor_tensor(fade[:, :], fade[:, :], apart[:, :], ALU.subtract))
                        c.then()
                        c.do("scalar", lambda e: e.activation(fade[:, :], fade[:, :], ACT.Exp))
                        c.do("vector", lambda e, cols=cols: e.tensor_tensor(table[:, cols], table[:, cols], gain[:, :], ALU.mult))
                        c.do("gpsimd", lambda e: e.tensor_tensor(total[:, :], total[:, :], gain[:, :], ALU.mult))
                        c.then()
                        c.do("vector", lambda e: e.tensor_tensor_scan(total[:, :], fade[:, :], total[:, :], carry[:, 0:1], ALU.mult, ALU.add))
                        first = 0.0 if r == 0 else table_last[:, 0:1]
                        if r == 0:
                            table_last = tensor(tmp, f"table_last{hop}", [P, 1])
                        c.do("vector", lambda e, cols=cols, first=first: e.tensor_tensor_scan(table[:, cols], fade[:, :], table[:, cols], first, ALU.mult, ALU.add))
                        c.then()
                        c.do("vector", lambda e: e.tensor_copy(carry[:, :], total[:, C - 1:C]))
                        c.do("vector", lambda e, r=r: e.tensor_copy(table_last[:, :], table[:, r * C + C - 1:r * C + C]))
                        c.do("scalar", lambda e: e.activation(least[:, 0:1], least[:, C:C + 1], ACT.Copy))
                        c.then()
                        c.do("vector", lambda e: e.reciprocal(total[:, :], total[:, :]))
                        c.then()
                        c.do("vector", lambda e, cols=cols: e.tensor_tensor(table[:, cols], table[:, cols], total[:, :], ALU.mult))
                    c.run()

                with ExitStack() as tmp:
                    node = tensor(tmp, f"node{hop}", [P, z.ntiles, z.D])
                    square = tensor(tmp, f"square{hop}", [P, z.ntiles, z.D])
                    rows_sb = tensor(tmp, f"rows_sb{hop}", [P, 4 * GROUP, P])
                    norm = tensor(tmp, f"norm{hop}", [P, z.ntiles])
                    entity = tensor(tmp, f"entity{hop}", [P, z.ntiles, z.D])
                    c = chain()
                    c.do("scalar", lambda e: e.dma_start(entity[:, :, :], entity_rows.rearrange("(p t) d -> p t d", p=P)), dma=True)
                    to_nodes(c, table, last_run, rows_sb, node)
                    wide = [P, z.ntiles, z.D]
                    c.then()
                    c.do("vector", lambda e: e.tensor_tensor(node[:, :, :], node[:, :, :], per_edge[:, :].unsqueeze(2).to_broadcast(wide), ALU.mult))
                    c.do("gpsimd", lambda e: e.tensor_tensor(result[:, :, :], result[:, :, :], entity[:, :, :], ALU.add))
                    c.then()
                    c.do("vector", lambda e: e.tensor_tensor(square[:, :, :], node[:, :, :], node[:, :, :], ALU.mult))
                    c.then()
                    c.do("vector", lambda e: e.tensor_reduce(norm[:, :], square[:, :, :], AX_X, ALU.add))
                    c.then()
                    c.do("vector", lambda e: e.tensor_scalar(norm[:, :], norm[:, :], 1e-24, None, ALU.max))
                    c.then()
                    c.do("scalar", lambda e: e.activation(norm[:, :], norm[:, :], ACT.Sqrt))
                    c.then()
                    c.do("vector", lambda e: e.reciprocal(norm[:, :], norm[:, :]))
                    c.then()
                    c.do("vector", lambda e: e.tensor_tensor(node[:, :, :], node[:, :, :], norm[:, :].unsqueeze(2).to_broadcast(wide), ALU.mult))
                    c.then()
                    c.do("sync", lambda e: e.dma_start(node_rows.rearrange("(p t) d -> p t d", p=P), node[:, :, :]), dma=True)
                    c.do("vector", lambda e: e.tensor_tensor(result[:, :, :], result[:, :, :], node[:, :, :], ALU.add))
                    if debug is not None and f"h{hop}" in debug:
                        c.then()
                        c.do("sync", lambda e: e.dma_start(debug[f"h{hop}"].rearrange("(p t) d -> p t d", p=P), node[:, :, :]), dma=True)
                    c.run()

        with ExitStack() as tmp:
            square = tensor(tmp, "square_last", [P, z.ntiles, z.D])
            col49 = tensor(tmp, "col_last", [P, z.ntiles])
            entity = tensor(tmp, "entity_last", [P, z.ntiles, z.D])
            c = chain()
            c.do("sync", lambda e: e.dma_start(entity[:, :, :], entity_rows.rearrange("(p t) d -> p t d", p=P)), dma=True)
            c.then()
            c.do("vector", lambda e: e.tensor_tensor(result[:, :, :], result[:, :, :], entity[:, :, :], ALU.add))
            layer_norm(c, result, square, col49, LN_EPS)
            c.then()
            c.do("sync", lambda e: e.dma_start(out[0:whole * z.ntiles, :].rearrange("(p t) d -> p t d", t=z.ntiles), result[0:whole, :, :]), dma=True)
            if odd:
                c.do("sync", lambda e: e.dma_start(out[whole * z.ntiles:z.N, :].unsqueeze(0), result[whole:whole + 1, 0:odd, :]), dma=True)
            c.run()


_INS = ["x", "src", "dst", "edge_type_64", "edge_weight", "L0_gnn_W1", "L0_gnn_b1", "L0_gnn_W2", "L0_gnn_b2",
        "L1_gnn_edge_emb", "L1_gnn_q_w", "L1_gnn_k_w"]


def kernel(**inputs):
    import numpy as _np
    import concourse.bacc as _bacc
    from concourse import mybir as _mybir
    from concourse.bass_utils import run_bass_kernel_spmd as _run

    nc = _bacc.Bacc("TRN2", target_bir_lowering=False, num_devices=1)
    arrays, args = {}, []
    for name in _INS:
        a = _np.ascontiguousarray(inputs[name])
        arrays[f"in_{name}_dram"] = a
        args.append(nc.dram_tensor(f"in_{name}_dram", a.shape, _mybir.dt.from_np(a.dtype), kind="ExternalInput").ap())
    shape = inputs["x"].shape
    out = nc.dram_tensor("out_0_dram", shape, _mybir.dt.float32, kind="ExternalOutput").ap()
    gnn_two_layers(nc, *args, out)
    r = _run(nc, [arrays], core_ids=[0])
    return r.results[0]["out_0_dram"]
```

```python
from contextlib import ExitStack, nullcontext
from math import ceil

import concourse.bass as bass
from concourse import mybir

ALU = mybir.AluOpType
ACT = mybir.ActivationFunctionType
AX_X = mybir.AxisListType.X
F32 = mybir.dt.float32
BF16 = mybir.dt.bfloat16
I32 = mybir.dt.int32

P = 128
BANK = 512
GROUP = BANK // P
UNROLL = 4
AHEAD = 2
HOPS = 3
LN_EPS = 1e-5
BIG = 1e30
START = 3e38
SKIP = 1.0e6


class Sizes:

    def __init__(self, nodes, edges, dim, types):
        self.N, self.E, self.D, self.T = nodes, edges, dim, types
        self.tiles = ceil(ceil(edges / P) / (GROUP * UNROLL)) * GROUP * UNROLL
        self.groups = self.tiles // GROUP
        self.tblocks = ceil(self.tiles / P)
        self.ntiles = ceil((nodes + 1) / P)
        self.NP = self.ntiles * P
        self.rblocks = ceil((nodes + 1 + self.tiles) / P)
        self.R = self.rblocks * P
        self.RW = self.R + P


class Sem:

    def __init__(self, handle):
        self.handle, self.base = handle, 0


class Chain:

    def __init__(self, nc, count, pool_count, only=None):
        self.nc, self.count, self.pool_count, self.stages = nc, count, pool_count, [[]]
        self.only = only or (lambda engine, name: nullcontext())

    def then(self):
        self.stages.append([])

    def do(self, engine, make, dma=False):
        self.stages[-1].append((engine, make, dma))

    def run(self):
        before, at, pool_at = [], self.count.base, self.pool_count.base
        for stage in self.stages:
            before.append((at, pool_at))
            for engine, _, dma in stage:
                if dma and engine == "gpsimd":
                    pool_at += 16
                else:
                    at += 16 if dma else 1
        before.append((at, pool_at))

        def play(name):
            def program(e):
                with self.only(e, name):
                    stages(e)

            def stages(e):
                seen, pool_seen = self.count.base, self.pool_count.base
                last = [[]] if name == "sync" else []
                for k, stage in enumerate(self.stages + last):
                    own = [s for s in stage if s[0] == name]
                    if not own and not (last and k == len(self.stages)):
                        continue
                    if before[k][0] > seen:
                        seen = before[k][0]
                        e.wait_ge(self.count.handle, seen)
                    if before[k][1] > pool_seen:
                        pool_seen = before[k][1]
                        e.wait_ge(self.pool_count.handle, pool_seen)
                    for _, make, dma in own:
                        s = self.pool_count if dma and name == "gpsimd" else self.count
                        make(e).then_inc(s.handle, 16 if dma else 1)

            return program

        with self.nc.Block() as block:
            for name in ("sync", "scalar", "vector", "tensor", "gpsimd"):
                getter = {"sync": block.sync, "scalar": block.scalar, "vector": block.vector,
                          "tensor": block.tensor, "gpsimd": block.gpsimd}[name]
                getter(play(name))
        self.count.base, self.pool_count.base = at, pool_at


class Step:

    def __init__(self, e, i, groups, turn=None, rates=None, spare=None):
        self.e, self.i, self.groups, self.turn = e, i, groups, turn
        self.rates, self.spare, self.used = rates, spare, 0

    def live(self, lag):
        return self.turn is not None or 0 <= self.i - lag < self.groups

    def slot(self, lag, ring):
        return (self.i - lag) % ring

    def at(self, f):
        if self.turn is None:
            return f(self.i)
        rate = f(self.i + UNROLL) - f(self.i)
        return self.turn * rate + f(self.i)

    def wait(self, *conditions, apart=False):
        found = []
        for s, f in conditions:
            if f(self.i) <= 0:
                assert self.turn is None
                continue
            if self.turn is None:
                found.append((s, s.base + f(self.i)))
                continue
            rate = f(self.i + UNROLL) - f(self.i)
            r = self.spare[self.used % len(self.spare)]
            self.used += 1
            self.e.reg_add(r, self.rates[rate], s.base + f(self.i) - rate)
            found.append((s, r))
        if apart and self.turn is not None:
            s, f = conditions[-1]
            self.e.wait_ge(s.handle, s.base + f(self.i))
        for s, value in found:
            self.e.wait_ge(s.handle, value)


def ring_count(lag, ring, inc):
    return lambda i: inc * ((i - lag) // ring + 1) if i >= lag else 0


def done(lag, per=1):
    return lambda i: per * (i - lag + 1) if i >= lag else 0


def pipeline(e, name, step, groups, depth, rates):
    first = ceil(depth / UNROLL) * UNROLL
    turns = (groups - first) // UNROLL
    for i in range(first):
        step(Step(e, i, groups))
    regs = {}
    for rate in rates:
        regs[rate] = e.alloc_register(f"{name}_rate{rate}")
        e.reg_mov(regs[rate], rate)
    spare = [e.alloc_register(f"{name}_until{n}") for n in range(8)]
    with e.Fori(0, turns) as turn:
        for b in range(UNROLL):
            step(Step(e, first + b, groups, turn, regs, spare))
        for rate in rates:
            e.reg_add(regs[rate], regs[rate], rate)
    for r in [*regs.values(), *spare]:
        e.free_register(r)
    for i in range(first + turns * UNROLL, groups + depth):
        step(Step(e, i, groups))


def gnn_two_layers(nc, x, src, dst, edge_type, edge_weight, w1, b1, w2, b2, edge_emb, q_w, k_w, out):
    z = Sizes(x.shape[0], src.shape[0], x.shape[1], edge_emb.shape[0])
    assert z.D == P and z.T * 2 == P and z.groups % UNROLL == 0
    top = ExitStack()
    with top:
        def sem(name):
            return Sem(top.enter_context(nc.semaphore(name)))

        def tensor(ctx, name, shape, dt=F32):
            return ctx.enter_context(nc.sbuf_tensor(name, shape, dt))

        def dram(name, shape, dt=F32):
            return nc.dram_tensor(name, shape, dt, kind="Internal").ap()

        banks_used = top.enter_context(nc.psum_tensor("banks", [P, 8, BANK], F32))
        bank = [banks_used[:, i, :] for i in range(8)]
        count, pool_count = sem("chain"), sem("chain_pool")

        def chain():
            return Chain(nc, count, pool_count)

        key_rows = dram("key_rows", (z.tblocks * P, 2, P))
        tile_rows = dram("tile_rows", (z.tblocks * P, 2, P), BF16)
        first_run = dram("first_run", (z.tblocks * P,), I32)
        node_words = dram("node_words", (3, P // 2, P))
        run_keys = dram("run_keys", (z.RW, 1))
        run_node = dram("run_node", (z.R,), I32)
        run_goes_on = dram("run_goes_on", (z.R,), BF16)
        run_out = dram("run_out", (z.R, z.D))
        run_sums = dram("run_sums", (z.R, z.D + 1))
        run_stats = dram("run_stats", (2, z.RW))
        node_rows = dram("node_rows", (z.NP, z.D))
        entity_rows = dram("entity_rows", (z.NP, z.D))
        by_dst = dram("by_dst", (P * z.tiles, 4))
        by_src = dram("by_src", (P * z.tiles, 4))

        ident = tensor(top, "ident", [P, P])
        below = tensor(top, "below", [P, P])
        above = tensor(top, "above", [P, P])
        ones = tensor(top, "ones", [P, P])
        column = tensor(top, "column", [P, P])
        row = tensor(top, "row", [P, 1])
        row_half = tensor(top, "row_half", [P, 1])
        c = chain()
        c.do("gpsimd", lambda e: e.memset(ones[:, :], 1.0))
        c.do("gpsimd", lambda e: e.iota(column[:, :], [[1, P]], base=0, channel_multiplier=0,
                                        allow_small_or_imprecise_dtypes=True))
        c.do("gpsimd", lambda e: e.iota(row[:, :], [[1, 1]], base=0, channel_multiplier=1,
                                        allow_small_or_imprecise_dtypes=True))
        c.then()
        c.do("vector", lambda e: e.tensor_scalar(ident[:, :], column[:, :], row[:, 0:1], None, ALU.is_equal))
        c.do("vector", lambda e: e.tensor_scalar(below[:, :], column[:, :], row[:, 0:1], None, ALU.is_lt))
        c.do("vector", lambda e: e.tensor_scalar(above[:, :], column[:, :], row[:, 0:1], None, ALU.is_gt))
        c.do("vector", lambda e: e.tensor_scalar(row_half[:, :], row[:, :], float(z.T), float(-z.T), ALU.is_ge, ALU.mult))
        c.then()
        c.do("vector", lambda e: e.tensor_tensor(row_half[:, :], row_half[:, :], row[:, :], ALU.add))
        c.run()

        def load_edges(c, to, array, skip=0):
            n = z.E - skip
            whole_rows = n // z.tiles
            c.do("sync", lambda e: e.dma_start(to[0:whole_rows, :], array[skip:skip + whole_rows * z.tiles].rearrange("(p k) -> p k", k=z.tiles)), dma=True)
            if n > whole_rows * z.tiles:
                c.do("sync", lambda e: e.dma_start(to[whole_rows:whole_rows + 1, 0:n - whole_rows * z.tiles],
                                                   array[skip + whole_rows * z.tiles:z.E].unsqueeze(0)), dma=True)

        def rows_of(c, columns, blocks, to):
            c.then()
            for b in range(blocks):
                c.do("tensor", lambda e, b=b: e.transpose(bank[b // GROUP][:, b % GROUP * P:b % GROUP * P + P],
                                                          columns[:, b * P:b * P + P], ident[:, :]))
            c.then()
            for b in range(0, blocks, GROUP):
                n = min(GROUP, blocks - b)
                engine = "vector" if b % (2 * GROUP) else "scalar"
                c.do(engine, copy(to[:, b:b + n, :], bank[b // GROUP][:, 0:n * P].rearrange("p (b q) -> p b q", b=n), engine))

        def copy(to, of, engine, scale=None):
            if engine == "scalar":
                return lambda e: e.activation(to, of, ACT.Copy, scale=1.0 if scale is None else scale)
            if scale is not None:
                return lambda e: e.tensor_scalar(to, of, scale, None, ALU.mult)
            return lambda e: e.tensor_copy(to, of)

        s_hot, s_hist = sem("s_hot"), sem("s_hist")
        s_copy_idx, s_weights, s_mm, s_write = sem("s_copy_idx"), sem("s_weights"), sem("s_mm"), sem("s_write")
        sp_gather = [sem(f"sp_gather{i}") for i in range(UNROLL)]
        sorted_count, sorted_pool_count = sem("sorted_chain"), sem("sorted_chain_pool")

        H = P // 2

        class Keys:

            def __init__(self, ctx, name, key_of, often_sorted=False):
                self.name, self.often_sorted = name, often_sorted
                self.low = tensor(ctx, f"{name}_low", [P, z.tblocks * P])
                self.high = tensor(ctx, f"{name}_high", [P, z.tblocks * P])
                self.key = tensor(ctx, f"{name}_key", [P, z.tblocks * P])
                self.hot_low = tensor(ctx, f"{name}_hot_low", [P, 2, GROUP, P], BF16)
                self.hot_high = tensor(ctx, f"{name}_hot_high", [P, 2, GROUP, H], BF16)
                self.hist = bank[7][0:H, 0:P]
                self.unsorted = tensor(ctx, f"{name}_unsorted", [1, 1], I32) if often_sorted else None
                low, high, key = self.low, self.high, self.key
                with ExitStack() as tmp:
                    raw = tensor(tmp, f"{name}_raw", [P, z.tiles], I32)
                    upper = tensor(tmp, f"{name}_upper", [P, z.tiles], I32)
                    turned = tensor(tmp, f"{name}_turned", [P, z.tblocks, P])
                    c = chain()
                    c.do("gpsimd", lambda e: e.memset(raw[:, :], z.N))
                    c.do("vector", lambda e: e.memset(key[:, :], float(z.N)))
                    c.do("vector", lambda e: e.memset(high[:, :], 0.0))
                    c.then()
                    load_edges(c, raw, key_of)
                    c.then()
                    c.do("vector", lambda e: e.tensor_copy(key[:, 0:z.tiles], raw[:, :]))
                    c.do("vector", lambda e: e.tensor_scalar(upper[:, :], raw[:, :], 7, None, ALU.arith_shift_right))
                    c.then()
                    c.do("vector", lambda e: e.tensor_scalar(raw[:, :], raw[:, :], P - 1, None, ALU.bitwise_and))
                    c.do("vector", lambda e: e.tensor_copy(high[:, 0:z.tiles], upper[:, :]))
                    c.then()
                    c.do("vector", lambda e: e.tensor_copy(low[:, 0:z.tiles], raw[:, :]))
                    for w, columns in ((0, key), (1, high)):
                        rows_of(c, columns, z.tblocks, turned)
                        c.then()
                        c.do("sync", lambda e, w=w: e.dma_start(key_rows.rearrange("(b t) w p -> w t b p", t=P)[w], turned[:, :, :]), dma=True)
                    if often_sorted:
                        following = tensor(tmp, f"{name}_following", [P, z.tiles])
                        falls = tensor(tmp, f"{name}_falls", [P, 1])
                        c.do("gpsimd", lambda e: e.memset(raw[:, :], z.N))
                        c.then()
                        load_edges(c, raw, key_of, skip=1)
                        c.then()
                        c.do("vector", lambda e: e.tensor_copy(following[:, :], raw[:, :]))
                        c.then()
                        c.do("vector", lambda e: e.tensor_tensor(following[:, :], key[:, 0:z.tiles], following[:, :], ALU.is_gt))
                        c.then()
                        c.do("vector", lambda e: e.tensor_reduce(falls[:, :], following[:, :], AX_X, ALU.max))
                        c.then()
                        c.do("tensor", lambda e: e.matmul(bank[6][0:1, 0:1], falls[:, :], ones[:, 0:1], start=True, stop=True))
                        c.then()
                        c.do("vector", lambda e: e.tensor_scalar(self.unsorted[:, :], bank[6][0:1, 0:1], 1.0, None, ALU.is_ge))
                    c.run()

            def hot_high_to(self, e, slot, cols):
                return e.tensor_tensor(self.hot_high[:, slot, :, :], column[:, 0:H].unsqueeze(1).to_broadcast([P, GROUP, H]),
                                       self.high[:, cols].unsqueeze(2).to_broadcast([P, GROUP, H]), ALU.is_equal)

            def hot_low_to(self, e, to, cols):
                return e.tensor_tensor(to, column[:, :].unsqueeze(1).to_broadcast([P, GROUP, P]),
                                       self.low[:, cols].unsqueeze(2).to_broadcast([P, GROUP, P]), ALU.is_equal)

            def vector_hist(self, s):
                if s.live(0):
                    cols = bass.ds(s.at(lambda i: GROUP * i), GROUP)
                    s.wait((s_hist, done(2)))
                    self.hot_low_to(s.e, self.hot_low[:, s.slot(0, 2), :, :], cols)
                    self.hot_high_to(s.e, s.slot(0, 2), cols).then_inc(s_hot.handle, 1)

            def tensor_hist(self, s, lag=0):
                if s.live(lag):
                    s.wait((s_hot, done(lag)))
                    for t in range(GROUP):
                        mm = s.e.matmul(self.hist, self.hot_high[:, s.slot(lag, 2), t, :], self.hot_low[:, s.slot(lag, 2), t, :],
                                        start=(s.turn is None and s.i == lag and t == 0), stop=True, skip_group_check=True)
                    mm.then_inc(s_hist.handle, 1)

            def counted(self):
                for s in (s_hot, s_hist):
                    s.base += z.groups

            def count(self):
                with nc.Block() as block:
                    @block.vector
                    def _(e):
                        pipeline(e, f"{self.name}_hv", self.vector_hist, z.groups, 2, (UNROLL,))

                    @block.tensor
                    def _(e):
                        pipeline(e, f"{self.name}_ht", self.tensor_hist, z.groups, 2, (UNROLL,))
                self.counted()

        def sort_edges(keys, key_of, other_of, third_of, third_dt, to):
            name, low, high, key, hot_high, often_sorted = keys.name, keys.low, keys.high, keys.key, keys.hot_high, keys.often_sorted
            s_place_hot, s_look, s_rank, s_math = (sem(f"{name}_s_{n}") for n in ("place_hot", "look", "rank", "math"))
            s_table, s_step, s_load = (sem(f"{name}_s_{n}") for n in ("table", "step", "load"))
            s_rows = [sem(f"{name}_s_rows{i}") for i in range(UNROLL)]
            sp_scatter = [sem(f"{name}_sp_scatter{i}") for i in range(UNROLL)]
            with ExitStack() as ctx:
                engine_types = {"sync": mybir.EngineType.SP, "scalar": mybir.EngineType.Activation, "vector": mybir.EngineType.DVE,
                           "tensor": mybir.EngineType.PE, "gpsimd": mybir.EngineType.Pool}

                def if_unsorted(e, engine, wanted=1):
                    if not often_sorted:
                        return nullcontext()
                    _, flag = nc.values_load_multi_w_load_instructions(keys.unsorted[0:1, 0:1], engines=[engine_types[engine]], min_val=0, max_val=1,
                                                                       skip_runtime_bounds_check_because="a comparison's result")
                    return e.If(flag[0] == wanted)

                words = tensor(ctx, f"{name}_words", [P, z.tiles, 4])
                raw_other = tensor(ctx, f"{name}_raw_other", [P, z.tiles], I32)
                raw_third = tensor(ctx, f"{name}_raw_third", [P, z.tiles], third_dt)
                counts = tensor(ctx, f"{name}_counts", [H, P])
                offsets = tensor(ctx, f"{name}_offsets", [H, P])

                a = tensor(ctx, f"{name}_a", [H, P])
                b = tensor(ctx, f"{name}_b", [H, P])
                nruns = tensor(ctx, f"{name}_nruns", [H, P])
                some = tensor(ctx, f"{name}_some", [H, P])
                ai = tensor(ctx, f"{name}_ai", [H, P], I32)
                bi = tensor(ctx, f"{name}_bi", [H, P], I32)

                def prefix(c, of, to):
                    c.then()
                    c.do("vector", lambda e: e.tensor_tensor_scan(to, ones[0:H, :], of, 0.0, ALU.mult, ALU.add))
                    c.then()
                    c.do("tensor", lambda e: e.matmul(bank[1][0:H, 0:1], above[0:H, 0:H], to[:, P - 1:P], start=True, stop=True))
                    c.then()
                    c.do("vector", lambda e: e.tensor_tensor(to, to, of, ALU.subtract))
                    c.then()
                    c.do("vector", lambda e: e.tensor_scalar(to, to, bank[1][0:H, 0:1], None, ALU.add))

                c = chain()
                c.do("vector", lambda e: e.tensor_copy(counts[:, :], keys.hist))
                prefix(c, counts[:, :], offsets[:, :])
                c.then()
                c.do("vector", lambda e: e.tensor_copy(ai[:, :], offsets[:, :]))
                c.do("vector", lambda e: e.tensor_tensor(a[:, :], offsets[:, :], counts[:, :], ALU.add))
                c.do("vector", lambda e: e.tensor_scalar(some[:, :], counts[:, :], 1.0, None, ALU.is_ge))
                c.then()
                c.do("vector", lambda e: e.tensor_scalar(bi[:, :], a[:, :], -1.0, None, ALU.add))
                c.do("vector", lambda e: e.tensor_scalar(ai[:, :], ai[:, :], 7, None, ALU.arith_shift_right))
                c.then()
                c.do("vector", lambda e: e.tensor_scalar(bi[:, :], bi[:, :], 7, None, ALU.arith_shift_right))
                c.do("vector", lambda e: e.tensor_copy(a[:, :], ai[:, :]))
                c.then()
                c.do("vector", lambda e: e.tensor_copy(b[:, :], bi[:, :]))
                c.then()
                c.do("vector", lambda e: e.tensor_tensor(b[:, :], b[:, :], a[:, :], ALU.subtract))
                c.then()
                c.do("vector", lambda e: e.scalar_tensor_tensor(nruns[:, :], b[:, :], 1.0, some[:, :], ALU.add, ALU.mult))
                prefix(c, nruns[:, :], a[:, :])
                c.then()
                c.do("vector", lambda e: e.tensor_scalar(some[:, :], some[:, :], -SKIP, SKIP, ALU.mult, ALU.add))
                c.then()
                c.do("vector", lambda e: e.tensor_tensor(a[:, :], a[:, :], some[:, :], ALU.add))
                c.then()
                c.do("vector", lambda e: e.scalar_tensor_tensor(b[:, :], a[:, :], -1.0, nruns[:, :], ALU.add, ALU.add))
                c.then()
                c.do("sync", lambda e: e.dma_start(node_words[0], counts[:, :]), dma=True)
                c.do("sync", lambda e: e.dma_start(node_words[1], a[:, :]), dma=True)
                c.do("sync", lambda e: e.dma_start(node_words[2], b[:, :]), dma=True)
                c.run()

                rows_in = tensor(ctx, f"{name}_rows_in", [P, UNROLL, GROUP, 2, P])
                hot_rows = tensor(ctx, f"{name}_hot_rows", [H, 2, GROUP, P])
                table = tensor(ctx, f"{name}_table", [H, 2, GROUP, P])
                waste = tensor(ctx, f"{name}_waste", [P, 2, GROUP, P])
                rank = tensor(ctx, f"{name}_rank", [P, 2, GROUP])
                base = tensor(ctx, f"{name}_base", [P, 2, GROUP])
                place = tensor(ctx, f"{name}_place", [P, 3, GROUP], I32)
                place_to = tensor(ctx, f"{name}_place_to", [P, UNROLL, GROUP], I32)
                load = tensor(ctx, f"{name}_load", [P, UNROLL, GROUP, 4])
                krows = key_rows.rearrange("t w p -> (t w p)")

                def loaded(only):
                    return Chain(nc, *((count, pool_count) if only is None else (sem(f"{name}_load_chain"), sem(f"{name}_load_chain_pool"))), only)

                c = loaded(if_unsorted if often_sorted else None)
                c.do("tensor", lambda e: e.matmul(bank[0][0:H, 0:P], ident[0:H, 0:H], offsets[:, :], start=True, stop=True))
                c.do("gpsimd", lambda e: e.memset(raw_other[:, :], 0))
                c.do("vector", lambda e: e.memset(raw_third[:, :], 0))
                c.do("vector", lambda e: e.memset(words[:, :, 3], 0.0))
                c.do("scalar", copy(words[:, :, 1], key[:, 0:z.tiles], "scalar"))
                c.then()
                load_edges(c, raw_other, other_of)
                load_edges(c, raw_third, third_of)
                c.then()
                c.do("vector", lambda e: e.tensor_copy(words[:, :, 0], raw_other[:, :]))
                c.do("vector", lambda e: e.tensor_copy(words[:, :, 2], raw_third[:, :]))
                c.run()

                def sync_rows(s):
                    if s.live(0):
                        at = s.at(lambda i: GROUP * 2 * P * i)
                        s.wait((s_rank, done(UNROLL)))
                        s.e.dma_start(rows_in[:, s.slot(0, UNROLL), :, :, :].rearrange("q t w p -> q (t w p)"),
                                      krows[bass.ds(at, GROUP * 2 * P)].partition_broadcast(P)).then_inc(s_rows[s.slot(0, UNROLL)].handle, 16)

                def vector_place(s):
                    e = s.e
                    if s.live(2):
                        g2, g4 = s.slot(2, 2), s.slot(2, UNROLL)
                        s.wait((s_look, done(2)), (s_math, done(3, 4)), (sp_scatter[g4], ring_count(2 + UNROLL, UNROLL, 16 * GROUP)))
                        for t in range(GROUP):
                            e.scalar_tensor_tensor(waste[:, 0, t, :], rows_in[:, g4, t, 0, :], key[:, bass.ds(s.at(lambda i, t=t: GROUP * (i - 2) + t), 1)],
                                                   below[:, :], ALU.is_equal, ALU.mult, accum_out=rank[:, g2, t:t + 1])
                            last = e.tensor_tensor_reduce(waste[:, 1, t, :], bank[2 + g2][:, t * P:t * P + P], hot_low_late[:, g4, t, :], 1.0, 0.0,
                                                          ALU.mult, ALU.add, base[:, g2, t:t + 1])
                        last.then_inc(s_rank.handle, 1)
                        s.wait((s_rank, done(2)))
                        e.tensor_tensor(place[:, 0, :], rank[:, g2, :], base[:, g2, :], ALU.add).then_inc(s_math.handle, 1)
                        s.wait((s_math, lambda i: 4 * (i - 2) + 1))
                        e.tensor_scalar(place[:, 1, :], place[:, 0, :], 7, None, ALU.arith_shift_right).then_inc(s_math.handle, 1)
                        e.tensor_scalar(place[:, 2, :], place[:, 0, :], P - 1, None, ALU.bitwise_and).then_inc(s_math.handle, 1)
                        s.wait((s_math, lambda i: 4 * (i - 2) + 3))
                        e.scalar_tensor_tensor(place_to[:, g4, :], place[:, 2, :], float(z.tiles), place[:, 1, :], ALU.mult, ALU.add)\
                            .then_inc(s_math.handle, 1)
                    if s.live(0):
                        g2, g4 = s.slot(0, 2), s.slot(0, UNROLL)
                        cols = bass.ds(s.at(lambda i: GROUP * i), GROUP)
                        s.wait((s_step, done(2, GROUP)), (s_look, done(2)), (s_rank, done(2)), (s_rows[g4], ring_count(0, UNROLL, 16)))
                        keys.hot_high_to(e, g2, cols)
                        keys.hot_low_to(e, hot_low_late[:, g4, :, :], cols)
                        e.tensor_scalar(hot_rows[:, g2, :, :], rows_in[0:H, g4, :, 1, :], row[0:H, 0:1], None, ALU.is_equal)\
                            .then_inc(s_place_hot.handle, 1)

                hot_low_late = tensor(ctx, f"{name}_hot_low_late", [P, UNROLL, GROUP, P], BF16)

                def scalar_table(s):
                    e = s.e
                    if s.live(1):
                        g2 = s.slot(1, 2)
                        for t in range(GROUP):
                            s.wait((s_step, lambda i, t=t: GROUP * (i - 1) + t), (s_look, done(3)))
                            e.activation(table[:, g2, t, :], bank[0][0:H, 0:P], ACT.Copy).then_inc(s_table.handle, 1)
                    if s.live(0):
                        g4 = s.slot(0, UNROLL)
                        s.wait((sp_scatter[g4], ring_count(UNROLL, UNROLL, 16 * GROUP)))
                        e.activation(load[:, g4, :, :].rearrange("p t w -> p (t w)"),
                                     words[:, :, :].rearrange("p k w -> p (k w)")[:, bass.ds(s.at(lambda i: 4 * GROUP * i), 4 * GROUP)],
                                     ACT.Copy).then_inc(s_load.handle, 1)

                def tensor_place(s):
                    e = s.e
                    if s.live(1):
                        g2, g4 = s.slot(1, 2), s.slot(1, UNROLL)
                        s.wait((s_place_hot, done(1)), (s_rank, done(3)))
                        for t in range(GROUP):
                            s.wait((s_table, lambda i, t=t: GROUP * (i - 1) + t + 1))
                            e.matmul(bank[0][0:H, 0:P], hot_high[:, g2, t, :], hot_low_late[:, g4, t, :],
                                     start=False, stop=True, skip_group_check=True).then_inc(s_step.handle, 1)
                            mm = e.matmul(bank[2 + g2][:, t * P:t * P + P], hot_rows[:, g2, t, :], table[:, g2, t, :], start=True, stop=True)
                        mm.then_inc(s_look.handle, 1)

                def pool_scatter(s):
                    if s.live(3):
                        g4 = s.slot(3, UNROLL)
                        s.wait((s_math, done(3, 4)), (s_load, done(3)), apart=True)
                        for t in range(GROUP):
                            s.e.indirect_dma_start(out=to, out_offset=bass.IndirectOffsetOnAxis(ap=place_to[:, g4, t:t + 1], axis=0),
                                                   in_=load[:, g4, t, :], in_offset=None).then_inc(sp_scatter[g4].handle, 16)

                with nc.Block() as block:
                    @block.sync
                    def _(e):
                        with if_unsorted(e, "sync"):
                            pipeline(e, f"{name}_ps", sync_rows, z.groups, UNROLL, (UNROLL,))

                    @block.vector
                    def _(e):
                        with if_unsorted(e, "vector"):
                            pipeline(e, f"{name}_pv", vector_place, z.groups, UNROLL + 2, (UNROLL, 16, 16 * GROUP))

                    @block.scalar
                    def _(e):
                        with if_unsorted(e, "scalar"):
                            pipeline(e, f"{name}_pa", scalar_table, z.groups, UNROLL, (UNROLL, GROUP * UNROLL, 16 * GROUP))

                    @block.tensor
                    def _(e):
                        with if_unsorted(e, "tensor"):
                            pipeline(e, f"{name}_pt", tensor_place, z.groups, UNROLL, (UNROLL, GROUP * UNROLL))

                    @block.gpsimd
                    def _(e):
                        with if_unsorted(e, "gpsimd"):
                            pipeline(e, f"{name}_pp", pool_scatter, z.groups, UNROLL, (UNROLL, GROUP * UNROLL))
                            for s in sp_scatter:
                                e.wait_ge(s.handle, s.base + 16 * z.tiles // UNROLL)

                if not often_sorted:
                    return
                in_rows = tensor(ctx, f"{name}_in_rows", [P, 3, z.tblocks, P], I32)
                as_float = tensor(ctx, f"{name}_as_float", [P, 3, z.tblocks, P])
                c = Chain(nc, sorted_count, sorted_pool_count, lambda e, engine: if_unsorted(e, engine, wanted=0))
                c.do("vector", lambda e: e.memset(in_rows[:, 0, :, :], 0))
                c.do("gpsimd", lambda e: e.memset(in_rows[:, 1, :, :], z.N))
                c.do("vector", lambda e: e.memset(in_rows[:, 2, :, :], 0))
                c.do("vector", lambda e: e.memset(words[:, :, 3], 0.0))
                c.then()
                for w, array in enumerate((other_of, key_of, third_of)):
                    to_rows = in_rows[:, w, :, :] if w < 2 else in_rows[:, w, :, :].bitcast(third_dt)
                    blocks, left = divmod(z.E, P * P)
                    if blocks:
                        c.do("sync", lambda e, to_rows=to_rows, array=array: e.dma_start(
                            to_rows[:, 0:blocks, :], array[0:blocks * P * P].rearrange("(b t q) -> t b q", t=P, q=P)), dma=True)
                    lines, left = divmod(left, P)
                    start = blocks * P * P
                    if lines:
                        c.do("sync", lambda e, to_rows=to_rows, array=array: e.dma_start(
                            to_rows[0:lines, blocks, :], array[start:start + lines * P].rearrange("(t q) -> t q", q=P)), dma=True)
                    if left:
                        c.do("sync", lambda e, to_rows=to_rows, array=array: e.dma_start(
                            to_rows[lines:lines + 1, blocks, 0:left], array[start + lines * P:z.E].unsqueeze(0)), dma=True)
                c.then()
                for w in range(3):
                    c.do("vector", lambda e, w=w: e.tensor_copy(as_float[:, w, :, :], in_rows[:, w, :, :] if w < 2 else in_rows[:, w, :, :].bitcast(third_dt)))
                for w in range(3):
                    first_bank = w % 2 * (z.tblocks + GROUP - 1) // GROUP
                    c.then()
                    for b in range(z.tblocks):
                        c.do("tensor", lambda e, w=w, b=b, first_bank=first_bank: e.transpose(
                            bank[first_bank + b // GROUP][:, b % GROUP * P:b % GROUP * P + P], as_float[:, w, b, :], ident[:, :]))
                    c.then()
                    for b in range(0, z.tblocks, GROUP):
                        n = min(GROUP * P, z.tiles - b * P)
                        engine = "vector" if b % (2 * GROUP) else "scalar"
                        c.do(engine, copy(words[:, b * P:b * P + n, w], bank[first_bank + b // GROUP][:, 0:n], engine))
                c.then()
                c.do("sync", lambda e: e.dma_start(to.rearrange("(p k) w -> p k w", p=P), words[:, :, :]), dma=True)
                c.run()

        def layout(ctx, name, of, third_rows):
            others = tensor(ctx, f"{name}_others", [P, z.tiles + AHEAD * GROUP], I32)
            weights = None if third_rows else tensor(ctx, f"{name}_weights", [P, z.tiles])
            q0 = tensor(ctx, f"{name}_q0", [1, z.tblocks * P], I32)
            cnt = tensor(ctx, f"{name}_cnt", [P, z.ntiles])
            last_run = tensor(ctx, f"{name}_last_run", [P, z.ntiles], I32)
            run_col = None if not third_rows else tensor(ctx, f"{name}_run_col", [P, z.rblocks], I32)
            within = None if third_rows else tensor(ctx, f"{name}_within", [P, z.tblocks * P])
            go_on = None if third_rows else tensor(ctx, f"{name}_go_on", [P, z.R], BF16)
            with ExitStack() as tmp:
                go_on = go_on or tensor(tmp, f"{name}_go_on", [P, z.R], BF16)
                words = tensor(tmp, f"{name}_sorted", [P, z.tiles, 4])
                col = tensor(tmp, f"{name}_col", [P, z.tblocks * P])
                turned = tensor(tmp, f"{name}_kt", [P, z.tblocks, P])
                flag = tensor(tmp, f"{name}_flag", [P, z.tblocks, P])
                inner = tensor(tmp, f"{name}_inner", [P, z.tblocks, P])
                number = tensor(tmp, f"{name}_number", [P, z.tblocks, P])
                half = tensor(tmp, f"{name}_half", [P, z.tblocks, 2, P], BF16)
                per = tensor(tmp, f"{name}_per", [P, z.tblocks])
                tot = tensor(tmp, f"{name}_tot", [P, z.tblocks])
                acc = tensor(tmp, f"{name}_acc", [P, z.tblocks])
                qi = tensor(tmp, f"{name}_qi", [P, z.tblocks], I32)
                node = tensor(tmp, f"{name}_node", [P, z.ntiles])
                nf = tensor(tmp, f"{name}_nf", [P, 2, z.ntiles])
                start_run = tensor(tmp, f"{name}_start_run", [P, z.ntiles], I32)
                minus = tensor(tmp, f"{name}_minus", [P, z.RW // P])
                keys = tensor(tmp, f"{name}_keys", [P, z.R])
                keyi = tensor(tmp, f"{name}_keyi", [1, z.R], I32)
                c = chain()
                c.do("sync", lambda e: e.dma_start(words[:, :, :], of.rearrange("(p k) w -> p k w", p=P)), dma=True)
                c.do("vector", lambda e: e.memset(col[:, :], float(z.N)))
                c.do("vector", lambda e: e.memset(inner[:, :, :], 1.0))
                c.do("vector", lambda e: e.memset(minus[:, :], -1.0))
                c.do("gpsimd", lambda e: e.iota(node[:, :], [[1, z.ntiles]], base=0, channel_multiplier=z.ntiles,
                                                allow_small_or_imprecise_dtypes=True))
                flat = node_words.rearrange("w a b -> w (a b)")
                c.do("sync", lambda e: e.dma_start(cnt[:, :], flat[0, 0:z.NP].rearrange("(p t) -> p t", p=P)), dma=True)
                c.do("sync", lambda e: e.dma_start(nf[:, :, :], flat[1:3, 0:z.NP].rearrange("w (p t) -> p w t", p=P)), dma=True)
                c.then()
                c.do("sync", lambda e: e.dma_start(run_keys.rearrange("(p k) w -> p (k w)", p=P), minus[:, :]), dma=True)
                c.do("vector", lambda e: e.tensor_copy(start_run[:, :], nf[:, 0, :]))
                c.do("vector", lambda e: e.tensor_copy(last_run[:, :], nf[:, 1, :]))
                c.do("vector", lambda e: e.tensor_copy(col[:, 0:z.tiles], words[:, :, 1]))
                c.do("vector", lambda e: e.tensor_copy(others[:, 0:z.tiles], words[:, :, 0]))
                c.do("gpsimd", lambda e: e.memset(others[:, z.tiles:], 0))
                if not third_rows:
                    c.do("vector", lambda e: e.tensor_copy(weights[:, :], words[:, :, 2]))
                c.do("gpsimd", lambda e: e.memset(inner[:, :, 0:1], 0.0))
                rows_of(c, col, z.tblocks, turned)
                for t in range(z.ntiles):
                    c.do("gpsimd", lambda e, t=t: e.indirect_dma_start(
                        out=run_keys, out_offset=bass.IndirectOffsetOnAxis(ap=start_run[:, t:t + 1], axis=0),
                        in_=node[:, t:t + 1], in_offset=None, bounds_check=z.RW - 1, oob_is_err=False), dma=True)
                c.then()
                c.do("vector", lambda e: e.memset(flag[:, :, 0:1], 1.0))
                c.do("vector", lambda e: e.tensor_tensor(flag[:, :, 1:P], turned[:, :, 1:P], turned[:, :, 0:P - 1], ALU.not_equal))
                c.do("sync", lambda e: e.dma_start(keys[:, :], run_keys.rearrange("r w -> (r w)")[0:z.R].partition_broadcast(P)), dma=True)
                c.then()
                c.do("vector", lambda e: e.tensor_tensor_scan(number[:, :, :].rearrange("p b q -> p (b q)"),
                                                              inner[:, :, :].rearrange("p b q -> p (b q)"),
                                                              flag[:, :, :].rearrange("p b q -> p (b q)"), 0.0, ALU.mult, ALU.add))
                c.do("vector", lambda e: e.tensor_scalar(go_on[:, :], keys[:, :], 0.0, None, ALU.is_lt))
                c.then()
                c.do("vector", lambda e: e.tensor_copy(per[:, :], number[:, :, P - 1]))
                c.then()
                c.do("tensor", lambda e: e.matmul(bank[4][:, 0:z.tblocks], above[:, :], per[:, :], start=True, stop=True))
                c.do("tensor", lambda e: e.matmul(bank[5][:, 0:z.tblocks], ones[:, :], per[:, :], start=True, stop=True))
                c.do("vector", lambda e: e.tensor_scalar(number[:, :, :], number[:, :, :], -1.0, None, ALU.add))
                c.then()
                c.do("vector", lambda e: e.tensor_copy(tot[:, :], bank[5][:, 0:z.tblocks]))
                c.do("vector", lambda e: e.tensor_copy(half[:, :, 1, :], number[:, :, :]))
                c.then()
                c.do("vector", lambda e: e.tensor_tensor_scan(acc[:, :], ones[:, 0:z.tblocks], tot[:, :], 0.0, ALU.mult, ALU.add))
                c.then()
                c.do("vector", lambda e: e.tensor_tensor(acc[:, :], acc[:, :], tot[:, :], ALU.subtract))
                c.then()
                c.do("vector", lambda e: e.tensor_tensor(qi[:, :], acc[:, :], bank[4][:, 0:z.tblocks], ALU.add))
                c.then()
                c.do("sync", lambda e: e.dma_start(first_run.rearrange("(b t) -> t b", t=P), qi[:, :], allow_slow_non_contiguous=True), dma=True)
                c.then()
                c.do("sync", lambda e: e.dma_start(q0[:, :], first_run.unsqueeze(0)), dma=True)
                if third_rows:
                    c.do("vector", lambda e: e.memset(col[:, :], 0.0))
                    c.do("vector", lambda e: e.tensor_tensor_scan(keys[0:1, :], keys[0:1, :], keys[0:1, :], -1.0, ALU.max, ALU.max))
                    c.then()
                    c.do("vector", lambda e: e.tensor_copy(col[:, 0:z.tiles], words[:, :, 2]))
                    c.do("vector", lambda e: e.tensor_copy(keyi[:, :], keys[0:1, :]))
                    rows_of(c, col, z.tblocks, turned)
                    c.then()
                    c.do("vector", lambda e: e.tensor_copy(half[:, :, 0, :], turned[:, :, :]))
                    c.do("sync", lambda e: e.dma_start(run_node.unsqueeze(0), keyi[:, :]), dma=True)
                    c.do("sync", lambda e: e.dma_start(run_goes_on.unsqueeze(0), go_on[0:1, :]), dma=True)
                    c.then()
                    c.do("sync", lambda e: e.dma_start(tile_rows.rearrange("(b t) w p -> t b w p", t=P), half[:, :, :, :]), dma=True)
                    c.do("sync", lambda e: e.dma_start(run_col[:, :], run_node.rearrange("(b r) -> r b", r=P), allow_slow_non_contiguous=True), dma=True)
                else:
                    c.then()
                    for b in range(z.tblocks):
                        c.do("tensor", lambda e, b=b: e.transpose(bank[b // GROUP][:, b % GROUP * P:b % GROUP * P + P], number[:, b, :], ident[:, :]))
                    c.then()
                    for b in range(0, z.tblocks, GROUP):
                        n = min(GROUP, z.tblocks - b)
                        c.do("vector", copy(within[:, b * P:(b + n) * P], bank[b // GROUP][:, 0:n * P], "vector"))
                c.run()
            return others, weights, q0, cnt, last_run, go_on, run_col, within

        def load_q0(s, e_type, q0, lag):
            _, values = nc.values_load_multi_w_load_instructions(
                q0[0:1, bass.ds(s.at(lambda i: GROUP * (i - lag)), GROUP)], engines=[e_type],
                min_val=0, max_val=z.R, skip_runtime_bounds_check_because="a prefix sum of run counts")
            return values

        def to_nodes(c, table, last_run, rows_sb, node):
            c.do("gpsimd", lambda e: e.memset(node[:, :, :], 0.0))
            per_round = 4 * GROUP
            for r in range(0, z.rblocks, per_round):
                n = min(per_round, z.rblocks - r)
                c.then()
                for b in range(n):
                    c.do("tensor", lambda e, b=b, r=r: e.transpose(bank[b // GROUP][:, b % GROUP * P:b % GROUP * P + P],
                                                                   table[:, (r + b) * P:(r + b) * P + P], ident[:, :]))
                c.then()
                for b in range(0, n, GROUP):
                    m = min(GROUP, n - b)
                    engine = "vector" if b % (2 * GROUP) else "scalar"
                    c.do(engine, copy(rows_sb[:, b:b + m, :], bank[b // GROUP][:, 0:m * P].rearrange("p (b q) -> p b q", b=m), engine))
                c.then()
                c.do("sync", lambda e, r=r, n=n: e.dma_start(run_out.rearrange("(b q) d -> q b d", q=P)[:, r:r + n, :], rows_sb[:, 0:n, :]), dma=True)
            gather_nodes(c, run_out, last_run, node)

        def gather_nodes(c, rows_of_runs, last_run, node):
            c.then()
            for t in range(z.ntiles):
                c.do("gpsimd", lambda e, t=t: e.indirect_dma_start(
                    out=node[:, t, :], out_offset=None, in_=rows_of_runs,
                    in_offset=bass.IndirectOffsetOnAxis(ap=last_run[:, t:t + 1], axis=0),
                    bounds_check=z.R - 1, oob_is_err=False), dma=True)

        def layer_norm(c, v, tmp, col, eps):
            def wide(a):
                return a.unsqueeze(2).to_broadcast([P, z.ntiles, z.D])
            c.then()
            c.do("vector", lambda e: e.tensor_reduce(col[:, :], v[:, :, :], AX_X, ALU.add))
            c.then()
            c.do("vector", lambda e: e.tensor_scalar(col[:, :], col[:, :], 1.0 / z.D, None, ALU.mult))
            c.then()
            c.do("vector", lambda e: e.tensor_tensor(v[:, :, :], v[:, :, :], wide(col[:, :]), ALU.subtract))
            c.then()
            c.do("vector", lambda e: e.tensor_tensor(tmp[:, :, :], v[:, :, :], v[:, :, :], ALU.mult))
            c.then()
            c.do("vector", lambda e: e.tensor_reduce(col[:, :], tmp[:, :, :], AX_X, ALU.add))
            c.then()
            c.do("vector", lambda e: e.tensor_scalar(col[:, :], col[:, :], 1.0 / z.D, eps, ALU.mult, ALU.add))
            c.then()
            c.do("scalar", lambda e: e.activation(col[:, :], col[:, :], ACT.Sqrt))
            c.then()
            c.do("vector", lambda e: e.reciprocal(col[:, :], col[:, :]))
            c.then()
            c.do("vector", lambda e: e.tensor_tensor(v[:, :, :], v[:, :, :], wide(col[:, :]), ALU.mult))

        with ExitStack() as ctx:
            dst_keys = Keys(ctx, "d", dst, often_sorted=True)
            dst_keys.count()
            sort_edges(dst_keys, dst, src, edge_weight, F32, by_dst)
        keys_ctx = ExitStack()
        src_keys = Keys(keys_ctx, "s", src)
        whole = z.N // z.ntiles
        odd = z.N - whole * z.ntiles
        with ExitStack() as ctx:
            others, weights, q0, cnt, last_run, go_on, _, within = layout(ctx, "l0", by_dst, False)
            table = tensor(ctx, "l0_table", [P, z.RW])
            nodes = tensor(ctx, "nodes", [P, z.ntiles, z.D])
            idx = tensor(ctx, "l0_idx", [P, UNROLL, GROUP], I32)
            rows = tensor(ctx, "l0_rows", [P, UNROLL, GROUP, z.D])
            spread = tensor(ctx, "l0_spread", [P, UNROLL, GROUP, P])
            w1_sb, w2_sb = tensor(ctx, "w1_sb", [P, P]), tensor(ctx, "w2_sb", [P, P])
            b1_sb, b2_sb = tensor(ctx, "b1_sb", [P, 1]), tensor(ctx, "b2_sb", [P, P])
            c = chain()
            c.do("vector", lambda e: e.memset(table[:, :], 0.0))
            c.do("gpsimd", lambda e: e.memset(nodes[:, :, :], 0.0))
            c.then()
            c.do("sync", lambda e: e.dma_start(nodes[0:whole, :, :], x[0:whole * z.ntiles, :].rearrange("(p t) d -> p t d", t=z.ntiles)), dma=True)
            if odd:
                c.do("sync", lambda e: e.dma_start(nodes[whole:whole + 1, 0:odd, :], x[whole * z.ntiles:z.N, :].unsqueeze(0)), dma=True)
            for sb, a in ((w1_sb[:, :], w1), (w2_sb[:, :], w2), (b1_sb[:, :], b1.unsqueeze(1)), (b2_sb[:, :], b2.partition_broadcast(P))):
                c.do("scalar", lambda e, sb=sb, a=a: e.dma_start(sb, a), dma=True)
            c.run()

            def pool_gather(idx, rows, table_rows, s_free):
                def program(s):
                    if s.live(0):
                        g4 = s.slot(0, UNROLL)
                        s.wait((s_free, done(UNROLL)), (s_copy_idx, done(0)), apart=True)
                        for t in range(GROUP):
                            s.e.indirect_dma_start(out=rows[:, g4, t, :], out_offset=None, in_=table_rows,
                                                   in_offset=bass.IndirectOffsetOnAxis(ap=idx[:, g4, t:t + 1], axis=0))\
                                .then_inc(sp_gather[g4].handle, 16)
                return program

            def copy_idx(s, idx, s_free):
                if s.turn is None and s.i == 0:
                    for g in range(AHEAD):
                        s.e.activation(idx[:, g, :], others[:, g * GROUP:(g + 1) * GROUP], ACT.Copy).then_inc(s_copy_idx.handle, 1)
                if s.live(0):
                    s.wait((s_free, done(UNROLL - AHEAD)))
                    s.e.activation(idx[:, s.slot(-AHEAD, UNROLL), :], others[:, bass.ds(s.at(lambda i: GROUP * (i + AHEAD)), GROUP)], ACT.Copy)\
                        .then_inc(s_copy_idx.handle, 1)

            def vector_l0(s):
                if s.live(0):
                    s.wait((s_mm, done(UNROLL)))
                    for t in range(GROUP):
                        col = bass.ds(s.at(lambda i, t=t: GROUP * i + t), 1)
                        last = s.e.tensor_scalar(spread[:, s.slot(0, UNROLL), t, :], column[:, :], within[:, col],
                                                 weights[:, col], ALU.is_equal, ALU.mult)
                    last.then_inc(s_weights.handle, 1)
                src_keys.vector_hist(s)

            def scalar_l0(s):
                copy_idx(s, idx, s_mm)
                if s.live(3):
                    q = load_q0(s, mybir.EngineType.Activation, q0, 3)
                    s.wait((s_mm, done(3)))
                    for t in range(GROUP):
                        s.wait((s_write, lambda i, t=t: GROUP * (i - 3) + t))
                        s.e.activation(table[:, bass.ds(q[t], P)], bank[s.slot(3, UNROLL)][:, t * P:t * P + P], ACT.Copy).then_inc(s_write.handle, 1)

            def tensor_l0(s):
                src_keys.tensor_hist(s, lag=1)
                if s.live(2):
                    s.wait((s_weights, done(2)), (sp_gather[s.slot(2, UNROLL)], ring_count(2, UNROLL, 16 * GROUP)), (s_write, done(2 + UNROLL, GROUP)))
                    for t in range(GROUP):
                        mm = s.e.matmul(bank[s.slot(2, UNROLL)][:, t * P:t * P + P], rows[:, s.slot(2, UNROLL), t, :],
                                        spread[:, s.slot(2, UNROLL), t, :], start=True, stop=True)
                    mm.then_inc(s_mm.handle, 1)

            with nc.Block() as block:
                @block.gpsimd
                def _(e):
                    pipeline(e, "gp", pool_gather(idx, rows, x, s_mm), z.groups, UNROLL, (UNROLL,))

                @block.scalar
                def _(e):
                    pipeline(e, "ga", scalar_l0, z.groups, UNROLL, (UNROLL, GROUP * UNROLL))

                @block.vector
                def _(e):
                    pipeline(e, "gv", vector_l0, z.groups, UNROLL, (UNROLL,))

                @block.tensor
                def _(e):
                    pipeline(e, "gt", tensor_l0, z.groups, UNROLL + 1, (UNROLL, 16 * GROUP, GROUP * UNROLL))
            src_keys.counted()
            s_copy_idx.base += z.groups + AHEAD
            for s in (s_mm, s_weights):
                s.base += z.groups
            s_write.base += z.tiles
            for s in sp_gather:
                s.base += 16 * z.tiles // UNROLL

            agg = tensor(ctx, "l0_agg", [P, z.ntiles, z.D])
            rows_sb = tensor(ctx, "l0_rows_sb", [P, 4 * GROUP, P])
            c = chain()
            c.do("vector", lambda e: e.tensor_tensor_scan(table[:, 0:z.R], go_on[:, :], table[:, 0:z.R], 0.0, ALU.mult, ALU.add))
            to_nodes(c, table, last_run, rows_sb, agg)
            c.then()
            c.do("vector", lambda e: e.tensor_tensor(agg[:, :, :], agg[:, :, :], nodes[:, :, :], ALU.add))
            c.then()
            c.do("gpsimd", lambda e: e.tensor_tensor(nodes[:, :, :], nodes[:, :, :], b2_sb[:, :].unsqueeze(1).to_broadcast([P, z.ntiles, z.D]), ALU.add))
            c.run()

            turned = tensor(ctx, "l0_turned", [P, 2, BANK])
            hidden = tensor(ctx, "l0_hidden", [P, 2, BANK])
            s_turn, s_turned, s_w1, s_hidden, s_w2, s_added = (sem(n) for n in ("s_turn", "s_turned", "s_w1", "s_hidden", "s_w2", "s_added"))
            node_groups = ceil(z.ntiles / GROUP)

            def tiles_of(g):
                return min(GROUP, z.ntiles - g * GROUP)

            def tensor_net(s):
                if s.live(0):
                    s.wait((s_turned, done(2)))
                    for t in range(tiles_of(s.i)):
                        mm = s.e.transpose(bank[s.i % 2][:, t * P:t * P + P], agg[:, s.i * GROUP + t, :], ident[:, :])
                    mm.then_inc(s_turn.handle, 1)
                if s.live(1):
                    g = s.i - 1
                    w = tiles_of(g) * P
                    s.wait((s_turned, done(1)), (s_hidden, done(3)))
                    s.e.matmul(bank[2 + g % 2][:, 0:w], w1_sb[:, :], turned[:, g % 2, 0:w], start=True, stop=True).then_inc(s_w1.handle, 1)
                if s.live(2):
                    g = s.i - 2
                    s.wait((s_hidden, done(2)), (s_added, done(4)))
                    for t in range(tiles_of(g)):
                        mm = s.e.matmul(bank[4 + g % 2][:, t * P:t * P + P], hidden[:, g % 2, t * P:t * P + P], w2_sb[:, :], start=True, stop=True)
                    mm.then_inc(s_w2.handle, 1)

            def scalar_net(s):
                if s.live(1):
                    g = s.i - 1
                    w = tiles_of(g) * P
                    s.wait((s_w1, done(1)), (s_w2, done(3)))
                    s.e.activation(hidden[:, g % 2, 0:w], bank[2 + g % 2][:, 0:w], ACT.Relu, bias=b1_sb[:, 0:1]).then_inc(s_hidden.handle, 1)

            def vector_net(s):
                if s.live(0):
                    w = tiles_of(s.i) * P
                    s.wait((s_turn, done(0)), (s_w1, done(2)))
                    s.e.tensor_copy(turned[:, s.i % 2, 0:w], bank[s.i % 2][:, 0:w]).then_inc(s_turned.handle, 1)
                if s.live(2):
                    g = s.i - 2
                    n = tiles_of(g)
                    s.wait((s_w2, done(2)))
                    s.e.tensor_tensor(nodes[:, g * GROUP:g * GROUP + n, :], nodes[:, g * GROUP:g * GROUP + n, :],
                                      bank[4 + g % 2][:, 0:n * P].rearrange("p (t d) -> p t d", t=n), ALU.add).then_inc(s_added.handle, 1)

            def net_steps(e, step):
                for i in range(node_groups + 2):
                    step(Step(e, i, node_groups))

            with nc.Block() as block:
                @block.tensor
                def _(e):
                    net_steps(e, tensor_net)

                @block.scalar
                def _(e):
                    net_steps(e, scalar_net)

                @block.vector
                def _(e):
                    net_steps(e, vector_net)
                    e.wait_ge(s_added.handle, node_groups)

            c = chain()
            row_sums = tensor(ctx, "l0_row_sums", [P, z.ntiles])
            layer_norm(c, nodes, agg, row_sums, LN_EPS)
            c.then()
            for to in (node_rows, entity_rows):
                c.do("sync", lambda e, to=to: e.dma_start(to.rearrange("(p t) d -> p t d", p=P), nodes[:, :, :]), dma=True)
            c.run()

        with keys_ctx:
            sort_edges(src_keys, src, dst, edge_type, I32, by_src)
        others, _, q0, cnt, last_run, _, run_col, _ = layout(top, "l1", by_src, True)
        per_edge = tensor(top, "per_edge", [P, z.ntiles])
        result = tensor(top, "result", [P, z.ntiles, z.D])
        q_sb, k_sb = tensor(top, "q_sb", [P, P]), tensor(top, "k_sb", [P, P])
        emb_hi_mid = tensor(top, "emb_hi_mid", [P, z.D], BF16)
        emb_lo = tensor(top, "emb_lo", [z.T, z.D], BF16)
        with ExitStack() as ctx:
            emb = tensor(ctx, "emb", [P, z.D])
            hi = tensor(ctx, "hi", [P, z.D], BF16)
            left = tensor(ctx, "left", [P, z.D])
            mid = tensor(ctx, "mid", [P, z.D], BF16)
            c = chain()
            c.do("vector", lambda e: e.memset(result[:, :, :], 0.0))
            c.do("sync", lambda e: e.dma_start(q_sb[:, :], q_w), dma=True)
            c.do("sync", lambda e: e.dma_start(k_sb[:, :], k_w), dma=True)
            c.do("sync", lambda e: e.dma_start(emb[0:z.T, :], edge_emb), dma=True)
            c.do("sync", lambda e: e.dma_start(emb[z.T:P, :], edge_emb), dma=True)
            c.then()
            c.do("vector", lambda e: e.tensor_copy(hi[:, :], emb[:, :]))
            c.do("vector", lambda e: e.tensor_scalar(cnt[:, :], cnt[:, :], 1.0, None, ALU.max))
            c.then()
            c.do("vector", lambda e: e.tensor_tensor(left[:, :], emb[:, :], hi[:, :], ALU.subtract))
            c.do("vector", lambda e: e.reciprocal(per_edge[:, :], cnt[:, :]))
            c.then()
            c.do("vector", lambda e: e.tensor_copy(mid[:, :], left[:, :]))
            c.then()
            c.do("vector", lambda e: e.tensor_copy(emb_hi_mid[0:z.T, :], hi[0:z.T, :]))
            c.do("vector", lambda e: e.tensor_copy(emb_hi_mid[z.T:P, :], mid[z.T:P, :]))
            c.do("vector", lambda e: e.tensor_tensor(emb_lo[:, :], left[0:z.T, :], mid[0:z.T, :], ALU.subtract))
            c.run()

        s_row = [sem(f"s_row{i}") for i in range(UNROLL)]
        s_win = [sem(f"s_win{i}") for i in range(UNROLL)]
        s_oht, s_rel, s_rt, s_rtt, s_rts = sem("s_oht"), sem("s_rel"), sem("s_rt"), sem("s_rtt"), sem("s_rts")
        s_kw, s_th, s_att, s_min, s_exp = sem("s_kw"), sem("s_th"), sem("s_att"), sem("s_min"), sem("s_exp")
        s_et, s_ets, s_acc = sem("s_et"), sem("s_ets"), sem("s_acc")
        trows = tile_rows.rearrange("t w p -> (t w p)")

        b_rel, b_rtt, b_kw, b_att, b_acc, b_st, b_et = range(7)
        for hop in range(HOPS):
            with ExitStack() as ctx:
                by_run = tensor(ctx, f"by_run{hop}", [P, 2, z.RW])
                table, stats = by_run[:, 0, :], by_run[0:2, 1, :]
                with ExitStack() as inner:
                    qt = tensor(inner, f"qt{hop}", [P, z.RW])
                    with ExitStack() as tmp:
                        heads = tensor(tmp, f"heads{hop}", [P, UNROLL, GROUP, z.D])
                        turned = tensor(tmp, f"headt{hop}", [P, 2, BANK])
                        blocks_of = ceil(z.rblocks / GROUP)

                        def blocks(g):
                            return min(GROUP, z.rblocks - g * GROUP)

                        def pool_q(s):
                            if s.live(0):
                                g4 = s.slot(0, UNROLL)
                                s.wait((s_rtt, done(UNROLL)))
                                for t in range(blocks(s.i)):
                                    s.e.indirect_dma_start(out=heads[:, g4, t, :], out_offset=None, in_=node_rows,
                                                           in_offset=bass.IndirectOffsetOnAxis(ap=run_col[:, s.i * GROUP + t:s.i * GROUP + t + 1], axis=0))\
                                        .then_inc(sp_gather[g4].handle, 16)

                        gathered = [sum(16 * blocks(g) for g in range(k, blocks_of, UNROLL)) for k in range(UNROLL)]

                        def tensor_q(s):
                            if s.live(0):
                                g4 = s.slot(0, UNROLL)
                                s.e.wait_ge(sp_gather[g4].handle, sp_gather[g4].base + sum(16 * blocks(g) for g in range(g4, s.i + 1, UNROLL)))
                                s.wait((s_rts, done(2)))
                                for t in range(blocks(s.i)):
                                    mm = s.e.transpose(bank[s.i % 2][:, t * P:t * P + P], heads[:, g4, t, :], ident[:, :])
                                mm.then_inc(s_rtt.handle, 1)
                            if s.live(1):
                                g, w = s.i - 1, blocks(s.i - 1) * P
                                s.wait((s_rts, done(1)), (s_th, done(3)))
                                s.e.matmul(bank[2 + g % 2][:, 0:w], q_sb[:, :], turned[:, g % 2, 0:w], start=True, stop=True).then_inc(s_kw.handle, 1)

                        def scalar_q(s):
                            if s.live(0):
                                w = blocks(s.i) * P
                                s.wait((s_rtt, done(0)), (s_kw, done(2)))
                                s.e.activation(turned[:, s.i % 2, 0:w], bank[s.i % 2][:, 0:w], ACT.Copy).then_inc(s_rts.handle, 1)

                        def vector_q(s):
                            if s.i == 0:
                                s.e.memset(qt[:, z.R:z.RW], 0.0)
                                s.e.memset(table, 0.0)
                                s.e.memset(by_run[:, 1, :], 1.0)
                                s.e.memset(bank[b_st], 0.0).then_inc(s_mm.handle, 1)
                            if s.live(0):
                                w = blocks(s.i) * P
                                s.wait((s_kw, done(0)))
                                s.e.tensor_scalar(qt[:, s.i * BANK:s.i * BANK + w], bank[2 + s.i % 2][:, 0:w], -1.0, None, ALU.mult).then_inc(s_th.handle, 1)

                        def all_steps(e, step):
                            for i in range(blocks_of + 1):
                                step(Step(e, i, blocks_of))

                        with nc.Block() as block:
                            @block.gpsimd
                            def _(e):
                                all_steps(e, pool_q)

                            @block.tensor
                            def _(e):
                                all_steps(e, tensor_q)

                            @block.scalar
                            def _(e):
                                all_steps(e, scalar_q)

                            @block.vector
                            def _(e):
                                all_steps(e, vector_q)
                                e.wait_ge(s_mm.handle, s_mm.base + 1)
                                e.wait_ge(s_th.handle, s_th.base + blocks_of)
                        for s in (s_rtt, s_rts, s_kw, s_th):
                            s.base += blocks_of
                        s_mm.base += 1
                        for s, n in zip(sp_gather, gathered):
                            s.base += n

                    idx = tensor(inner, f"idx{hop}", [P, UNROLL, GROUP], I32)
                    tails = tensor(inner, f"tails{hop}", [P, UNROLL, GROUP, z.D])
                    rows_in = tensor(inner, f"rows_in{hop}", [P, UNROLL, GROUP, 2, P], BF16)
                    window = tensor(inner, f"window{hop}", [P, UNROLL, GROUP, P])
                    hot_type = tensor(inner, f"hot_type{hop}", [P, 2, GROUP, P], BF16)
                    mask = tensor(inner, f"mask{hop}", [P, UNROLL, GROUP, P], BF16)
                    rt = tensor(inner, f"rt{hop}", [P, UNROLL, GROUP, z.D])
                    rtt = tensor(inner, f"rtt{hop}", [P, 2, BANK])
                    right = tensor(inner, f"right{hop}", [P, 2, BANK])
                    att = tensor(inner, f"att{hop}", [P, 2, GROUP, P])
                    stat = tensor(inner, f"stat{hop}", [P, 2, GROUP, 2])
                    weight = tensor(inner, f"weight{hop}", [P, 2, GROUP, P])
                    weight_t = tensor(inner, f"weight_t{hop}", [P, 2, GROUP, P])

                    def sync_hop(s):
                        if not s.live(0):
                            return
                        g4 = s.slot(0, UNROLL)
                        at = s.at(lambda i: GROUP * 2 * P * i)
                        q = load_q0(s, mybir.EngineType.SP, q0, 0)
                        s.wait((s_oht, done(UNROLL)))
                        s.e.dma_start(rows_in[:, g4, :, :, :].rearrange("q t w p -> q (t w p)"),
                                      trows[bass.ds(at, GROUP * 2 * P)].partition_broadcast(P)).then_inc(s_row[g4].handle, 16)
                        s.wait((s_att, done(UNROLL)))
                        for t in range(GROUP):
                            s.e.dma_start(window[:, g4, t, :], qt[:, bass.ds(q[t], P)]).then_inc(s_win[g4].handle, 16)

                    def vector_hop(s):
                        e = s.e
                        def write(t):
                            if s.live(5):
                                s.wait((s_write, lambda i: GROUP * (i - 5) + t))
                                e.tensor_copy(by_run[:, :, bass.ds(q[t], P)], banks_used[:, b_acc:b_st + 1, t * P:t * P + P]).then_inc(s_write.handle, 1)

                        def least_of(t):
                            if s.live(3):
                                g2, g4 = s.slot(3, 2), s.slot(3, UNROLL)
                                e.tensor_tensor_reduce(att[:, g2, t, :], bank[b_att][:, t * P:t * P + P], mask[:, g4, t, :],
                                                       1.0, START, ALU.add, ALU.min, stat[:, g2, t, 0:1]).then_inc(s_min.handle, 1)

                        if s.live(5):
                            q = load_q0(s, mybir.EngineType.DVE, q0, 5)
                            s.wait((s_acc, done(5)))
                        write(0)
                        if s.live(1):
                            g4 = s.slot(1, UNROLL)
                            s.wait((s_rel, done(1)), (sp_gather[g4], ring_count(1, UNROLL, 16 * GROUP)))
                            e.tensor_tensor(rt[:, g4, :, :].rearrange("p t d -> p (t d)"), bank[b_rel][:, :],
                                            tails[:, g4, :, :].rearrange("p t d -> p (t d)"), ALU.mult).then_inc(s_rt.handle, 1)
                        write(1)
                        if s.live(3):
                            s.wait((s_att, done(3)), apart=True)
                        least_of(0)
                        write(2)
                        least_of(1)
                        write(3)
                        least_of(2)
                        least_of(3)
                        if s.live(0):
                            g2, g4 = s.slot(0, 2), s.slot(0, UNROLL)
                            s.wait((s_row[g4], ring_count(0, UNROLL, 16)), (s_rel, done(2)), (s_min, done(4, GROUP)))
                            e.tensor_scalar(hot_type[:, g2, :, :], rows_in[:, g4, :, 0, :], row_half[:, 0:1], None, ALU.is_equal)
                            e.tensor_scalar(mask[:, g4, :, :], rows_in[:, g4, :, 1, :], row[:, 0:1], BIG, ALU.not_equal, ALU.mult)\
                                .then_inc(s_oht.handle, 1)

                    def tensor_hop(s):
                        e = s.e
                        if s.live(1):
                            g2 = s.slot(1, 2)
                            s.wait((s_oht, done(1)), (s_rt, done(2)))
                            for t in range(GROUP):
                                e.matmul(bank[b_rel][:, t * P:t * P + P], hot_type[:, g2, t, :], emb_hi_mid[:, :], start=True, stop=False)
                                mm = e.matmul(bank[b_rel][:, t * P:t * P + P], hot_type[0:z.T, g2, t, :], emb_lo[:, :], start=False, stop=True)
                            mm.then_inc(s_rel.handle, 1)
                        if s.live(3):
                            g2, g4 = s.slot(3, 2), s.slot(3, UNROLL)
                            s.wait((s_th, done(3)), (s_win[g4], ring_count(3, UNROLL, 16 * GROUP)), (s_min, done(4, GROUP)))
                            for t in range(GROUP):
                                mm = e.matmul(bank[b_att][:, t * P:t * P + P], window[:, g4, t, :], right[:, g2, t * P:t * P + P], start=True, stop=True)
                            mm.then_inc(s_att.handle, 1)
                        if s.live(4):
                            g2 = s.slot(4, 2)
                            s.wait((s_exp, done(4, GROUP)), (s_ets, done(5)))
                            for t in range(GROUP):
                                mm = e.transpose(bank[b_et][:, t * P:t * P + P], weight[:, g2, t, :], ident[:, :])
                            mm.then_inc(s_et.handle, 1)
                        if s.live(2):
                            s.wait((s_rts, done(2)), (s_th, done(3)))
                            e.matmul(bank[b_kw][:, :], k_sb[:, :], rtt[:, s.slot(2, 2), :], start=True, stop=True).then_inc(s_kw.handle, 1)
                        if s.live(1):
                            s.wait((s_rt, done(1)), (s_rts, done(2)))
                            for t in range(GROUP):
                                mm = e.transpose(bank[b_rtt][:, t * P:t * P + P], rt[:, s.slot(1, UNROLL), t, :], ident[:, :])
                            mm.then_inc(s_rtt.handle, 1)
                        if s.live(4):
                            s.wait((s_ets, done(4)), (s_write, done(5, GROUP)))
                            for t in range(GROUP):
                                e.transpose(bank[b_st][0:2, t * P:t * P + P], stat[:, s.slot(4, 2), t, :], ident[:, :])
                                mm = e.matmul(bank[b_acc][:, t * P:t * P + P], rt[:, s.slot(4, UNROLL), t, :], weight_t[:, s.slot(4, 2), t, :],
                                              start=True, stop=True)
                            mm.then_inc(s_acc.handle, 1)

                    def scalar_hop(s):
                        e = s.e
                        copy_idx(s, idx, s_rt)
                        if s.live(4):
                            s.wait((s_et, done(4)), (s_acc, done(6)))
                            e.activation(weight_t[:, s.slot(4, 2), :, :].rearrange("p t d -> p (t d)"), bank[b_et][:, :], ACT.Copy).then_inc(s_ets.handle, 1)
                        if s.live(2):
                            s.wait((s_kw, done(2)))
                            e.activation(right[:, s.slot(2, 2), :], bank[b_kw][:, :], ACT.Tanh).then_inc(s_th.handle, 1)
                        if s.live(1):
                            s.wait((s_rtt, done(1)))
                            e.activation(rtt[:, s.slot(1, 2), :], bank[b_rtt][:, :], ACT.Copy).then_inc(s_rts.handle, 1)
                        if s.live(3):
                            g2 = s.slot(3, 2)
                            for t in range(GROUP):
                                s.wait((s_min, lambda i, t=t: GROUP * (i - 3) + t + 1))
                                e.activation(weight[:, g2, t, :], att[:, g2, t, :], ACT.Exp, scale=-1.0, bias=stat[:, g2, t, 0:1],
                                             accum_out=stat[:, g2, t, 1:2]).then_inc(s_exp.handle, 1)

                    deep = 2 * UNROLL
                    with nc.Block() as block:
                        @block.sync
                        def _(e):
                            pipeline(e, f"hs{hop}", sync_hop, z.groups, deep, (UNROLL,))

                        @block.gpsimd
                        def _(e):
                            pipeline(e, f"hp{hop}", pool_gather(idx, tails, node_rows, s_rt), z.groups, deep, (UNROLL,))

                        @block.vector
                        def _(e):
                            pipeline(e, f"hd{hop}", vector_hop, z.groups, deep, (UNROLL, GROUP * UNROLL, 16 * GROUP))

                        @block.tensor
                        def _(e):
                            pipeline(e, f"he{hop}", tensor_hop, z.groups, deep, (UNROLL, GROUP * UNROLL, 16 * GROUP))

                        @block.scalar
                        def _(e):
                            pipeline(e, f"ha{hop}", scalar_hop, z.groups, deep, (UNROLL, GROUP * UNROLL))
                    s_copy_idx.base += z.groups + AHEAD
                    for s in (s_oht, s_rel, s_rt, s_rtt, s_rts, s_kw, s_th, s_att, s_et, s_ets, s_acc):
                        s.base += z.groups
                    for s in (s_write, s_min, s_exp):
                        s.base += z.tiles
                    for s in s_row:
                        s.base += 16 * z.groups // UNROLL
                    for s in (*s_win, *sp_gather):
                        s.base += 16 * z.tiles // UNROLL

                with ExitStack() as tmp:
                    parts = ceil(z.rblocks / 10)
                    per_part = ceil(z.rblocks / parts)
                    C = per_part * P
                    behind = 3
                    low = tensor(tmp, f"low{hop}", [P, 2, C])
                    total = tensor(tmp, f"total{hop}", [P, 3, C])
                    go_on = tensor(tmp, f"go_on{hop}", [P, 2, C], BF16)
                    least = tensor(tmp, f"least{hop}", [P, C + 1])
                    fade = tensor(tmp, f"fade{hop}", [P, 2, C])
                    gain = tensor(tmp, f"gain{hop}", [P, 2, C])
                    apart = tensor(tmp, f"apart{hop}", [P, 2, C])
                    last = tensor(tmp, f"last{hop}", [P, 2])
                    rows_sb = tensor(tmp, f"rows_sb{hop}", [P, per_part, z.D + 1])
                    sum_bank = ceil(per_part / GROUP)

                    def stages_of(r):
                        g, h, n = r % 2, r % 3, min(per_part, z.rblocks - r * per_part)
                        w = n * P
                        cols = slice(r * C, r * C + w)
                        return [
                            [("sync", lambda e: e.dma_start(low[:, g, 0:w], run_stats[0, cols].partition_broadcast(P)), True),
                             ("scalar", lambda e: e.dma_start(total[:, h, 0:w], run_stats[1, cols].partition_broadcast(P)), True),
                             ("sync", lambda e: e.dma_start(go_on[:, g, 0:w], run_goes_on[cols].partition_broadcast(P)), True)],
                            [("vector", lambda e: e.tensor_scalar(apart[:, g, 0:w], go_on[:, g, 0:w], -BIG, BIG, ALU.mult, ALU.add), False)],
                            [("vector", lambda e: e.tensor_tensor_scan(least[:, 1:w + 1], apart[:, g, 0:w], low[:, g, 0:w], least[:, 0:1], ALU.add, ALU.min), False)],
                            [("vector", lambda e: e.tensor_tensor(gain[:, g, 0:w], least[:, 1:w + 1], low[:, g, 0:w], ALU.subtract), False),
                             ("vector", lambda e: e.tensor_tensor(fade[:, g, 0:w], least[:, 1:w + 1], least[:, 0:w], ALU.subtract), False)],
                            [("scalar", lambda e: e.activation(gain[:, g, 0:w], gain[:, g, 0:w], ACT.Exp), False),
                             ("scalar", lambda e: e.activation(least[:, 0:1], least[:, w:w + 1], ACT.Copy), False),
                             ("vector", lambda e: e.tensor_tensor(fade[:, g, 0:w], fade[:, g, 0:w], apart[:, g, 0:w], ALU.subtract), False)],
                            [("scalar", lambda e: e.activation(fade[:, g, 0:w], fade[:, g, 0:w], ACT.Exp), False),
                             ("vector", lambda e: e.tensor_tensor(table[:, cols], table[:, cols], gain[:, g, 0:w], ALU.mult), False),
                             ("gpsimd", lambda e: e.tensor_tensor(total[:, h, 0:w], total[:, h, 0:w], gain[:, g, 0:w], ALU.mult), False)],
                            [("vector", lambda e: e.tensor_tensor_scan(total[:, h, 0:w], fade[:, g, 0:w], total[:, h, 0:w], last[:, 0:1], ALU.mult, ALU.add), False),
                             ("vector", lambda e: e.tensor_tensor_scan(table[:, cols], fade[:, g, 0:w], table[:, cols], last[:, 1:2], ALU.mult, ALU.add), False)],
                            [("vector", lambda e: e.tensor_copy(last[:, 0:1], total[:, h, w - 1:w]), False),
                             ("vector", lambda e: e.tensor_copy(last[:, 1:2], table[:, r * C + w - 1:r * C + w]), False),
                             *(("tensor", lambda e, b=b: e.transpose(bank[b // GROUP][:, b % GROUP * P:b % GROUP * P + P],
                                                                     table[:, r * C + b * P:r * C + b * P + P], ident[:, :]), False) for b in range(n)),
                             *(("tensor", lambda e, b=b: e.transpose(bank[sum_bank][:, b:b + 1], total[0:1, h, b * P:b * P + P], ident[0:1, 0:1]), False)
                               for b in range(n))],
                            [*(("scalar" if b else "vector",
                                copy(rows_sb[:, b:min(b + GROUP, n), 0:z.D],
                                     bank[b // GROUP][:, 0:(min(b + GROUP, n) - b) * P].rearrange("p (b q) -> p b q", q=P), "scalar" if b else "vector"), False)
                               for b in range(0, n, GROUP)),
                             ("vector", lambda e: e.tensor_copy(rows_sb[:, 0:n, z.D], bank[sum_bank][:, 0:n]), False)],
                            [("sync", lambda e: e.dma_start(run_sums.rearrange("(b q) d -> q b d", q=P)[:, r * per_part:r * per_part + n, :],
                                                            rows_sb[:, 0:n, :]), True)],
                        ]

                    c = chain()
                    c.do("sync", lambda e: e.dma_start(run_stats, stats), dma=True)
                    c.do("vector", lambda e: e.memset(least[:, 0:1], BIG))
                    c.do("vector", lambda e: e.memset(last[:, :], 0.0))
                    lists = [stages_of(r) for r in range(parts)]
                    for k in range(len(lists[0]) + behind * (parts - 1)):
                        c.then()
                        for r in range(parts):
                            if 0 <= k - behind * r < len(lists[r]):
                                for engine, make, dma in lists[r][k - behind * r]:
                                    c.do(engine, make, dma=dma)
                    c.run()

                with ExitStack() as tmp:
                    node = tensor(tmp, f"node{hop}", [P, z.ntiles, z.D + 1])
                    square = tensor(tmp, f"square{hop}", [P, z.ntiles, z.D])
                    norm = tensor(tmp, f"norm{hop}", [P, z.ntiles])
                    scale = tensor(tmp, f"scale{hop}", [P, z.ntiles])
                    sums = node[:, :, 0:z.D]
                    c = chain()
                    c.do("vector", lambda e: e.memset(node[:, :, :], 0.0))
                    gather_nodes(c, run_sums, last_run, node)
                    c.then()
                    c.do("vector", lambda e: e.tensor_tensor(square[:, :, :], sums, sums, ALU.mult))
                    c.do("vector", lambda e: e.tensor_scalar(scale[:, :], node[:, :, z.D], 1.0, None, ALU.max))
                    c.then()
                    c.do("vector", lambda e: e.tensor_reduce(norm[:, :], square[:, :, :], AX_X, ALU.add))
                    c.do("vector", lambda e: e.reciprocal(scale[:, :], scale[:, :]))
                    c.then()
                    c.do("vector", lambda e: e.tensor_tensor(scale[:, :], scale[:, :], per_edge[:, :], ALU.mult))
                    c.then()
                    c.do("vector", lambda e: e.tensor_tensor(norm[:, :], norm[:, :], scale[:, :], ALU.mult))
                    c.then()
                    c.do("vector", lambda e: e.tensor_tensor(norm[:, :], norm[:, :], scale[:, :], ALU.mult))
                    c.then()
                    c.do("vector", lambda e: e.tensor_scalar(norm[:, :], norm[:, :], 1e-24, None, ALU.max))
                    c.then()
                    c.do("scalar", lambda e: e.activation(norm[:, :], norm[:, :], ACT.Sqrt))
                    c.then()
                    c.do("vector", lambda e: e.reciprocal(norm[:, :], norm[:, :]))
                    c.then()
                    c.do("vector", lambda e: e.tensor_tensor(scale[:, :], scale[:, :], norm[:, :], ALU.mult))
                    c.then()
                    c.do("vector", lambda e: e.tensor_tensor(square[:, :, :], sums, scale[:, :].unsqueeze(2).to_broadcast([P, z.ntiles, z.D]), ALU.mult))
                    c.then()
                    c.do("sync", lambda e: e.dma_start(node_rows.rearrange("(p t) d -> p t d", p=P), square[:, :, :]), dma=True)
                    c.do("vector", lambda e: e.tensor_tensor(result[:, :, :], result[:, :, :], square[:, :, :], ALU.add))
                    c.run()

        with ExitStack() as tmp:
            square = tensor(tmp, "square_last", [P, z.ntiles, z.D])
            row_sums = tensor(tmp, "row_sums_last", [P, z.ntiles])
            entity = tensor(tmp, "entity_last", [P, z.ntiles, z.D])
            c = chain()
            c.do("sync", lambda e: e.dma_start(entity[:, :, :], entity_rows.rearrange("(p t) d -> p t d", p=P)), dma=True)
            c.then()
            c.do("vector", lambda e: e.scalar_tensor_tensor(result[:, :, :], entity[:, :, :], float(HOPS + 1), result[:, :, :], ALU.mult, ALU.add))
            layer_norm(c, result, square, row_sums, LN_EPS)
            c.then()
            c.do("sync", lambda e: e.dma_start(out[0:whole * z.ntiles, :].rearrange("(p t) d -> p t d", t=z.ntiles), result[0:whole, :, :]), dma=True)
            if odd:
                c.do("sync", lambda e: e.dma_start(out[whole * z.ntiles:z.N, :].unsqueeze(0), result[whole:whole + 1, 0:odd, :]), dma=True)
            c.run()


_INS = ["x", "src", "dst", "edge_type_64", "edge_weight", "L0_gnn_W1", "L0_gnn_b1", "L0_gnn_W2", "L0_gnn_b2",
        "L1_gnn_edge_emb", "L1_gnn_q_w", "L1_gnn_k_w"]


def kernel(**inputs):
    import numpy as _np
    import concourse.bacc as _bacc
    from concourse import mybir as _mybir
    from concourse.bass_utils import run_bass_kernel_spmd as _run

    nc = _bacc.Bacc("TRN2", target_bir_lowering=False, num_devices=1)
    arrays, args = {}, []
    for name in _INS:
        a = _np.ascontiguousarray(inputs[name])
        arrays[f"in_{name}_dram"] = a
        args.append(nc.dram_tensor(f"in_{name}_dram", a.shape, _mybir.dt.from_np(a.dtype), kind="ExternalInput").ap())
    shape = inputs["x"].shape
    out = nc.dram_tensor("out_0_dram", shape, _mybir.dt.float32, kind="ExternalOutput").ap()
    gnn_two_layers(nc, *args, out)
    r = _run(nc, [arrays], core_ids=[0])
    return r.results[0]["out_0_dram"]
```
